# Optimizing a Trainium2 kernel written in Bass

```python
import numpy as np
import jax
import jax.numpy as jnp

def _softmax(x, axis=-1):
    return jax.nn.softmax(x, axis=axis)

def _gelu(x):
    return jax.nn.gelu(x, approximate=True)

def _silu(x):
    return jax.nn.silu(x)

def _sigmoid(x):
    return jax.nn.sigmoid(x)

def _layernorm(x, axis=-1, eps=1e-05):
    m = jnp.mean(x, axis=axis, keepdims=True)
    v = jnp.var(x, axis=axis, keepdims=True)
    return (x - m) / jnp.sqrt(v + eps)

def _scatter_add(tgt, idx, src, axis=0):
    return tgt.at[idx].add(src)

def _segment_sum(src, seg, n):
    return jax.ops.segment_sum(src, seg, n)
kernel_name = 'mk_flamingo_gated_d1_seqx_r4_1353f3'

def setup_inputs(seed: int=0):
    np.random.seed(seed)
    _w = jnp.asarray

    def _rec_inputs():
        import jax
        import jax.numpy as jnp
        _rk = jax.random.key(seed)
        x = -0.0002928 + 1 * jax.random.normal(jax.random.fold_in(_rk, 1), (16, 112, 256), jnp.float32)
        _lenS = 112 - jax.random.randint(jax.random.fold_in(_rk, 7), (16,), 0, max(1, 112 // 4) + 1, jnp.int32)
        _lenS2 = 375 - jax.random.randint(jax.random.fold_in(_rk, 8), (16,), 0, max(1, 375 // 4) + 1, jnp.int32)
        _ctx_1024P = jax.random.normal(jax.random.fold_in(_rk, 11), (16, 16, 256), jnp.float32)
        _ctx_1024c = jax.random.dirichlet(jax.random.fold_in(_rk, 511), 0.3 * jnp.ones((16,), jnp.float32), (16, 375))
        _ctx_1024t = jnp.einsum('bsk,bkd->bsd', _ctx_1024c, _ctx_1024P)
        _ctx_1024t = _ctx_1024t * jax.lax.rsqrt(jnp.mean(jnp.square(_ctx_1024t)) + 1e-12) * 0.953939
        ctx_1024 = -1.39393e-06 + 0.999914 * (_ctx_1024t + 0.3 * jax.random.normal(jax.random.fold_in(_rk, 611), (16, 375, 256), jnp.float32))
        _g = jax.random.normal(jax.random.fold_in(_rk, 9001), (2, 1), jnp.float32)
        _g = jnp.sign(_g) * jnp.maximum(jnp.abs(_g), 1.0) + (_g == 0) * 1.0
        g_xattn = _g[0]
        g_ffn = _g[1]
        return (x, ctx_1024, g_xattn, g_ffn)
    x, ctx_1024, g_xattn, g_ffn = _rec_inputs()

    def _L0_xattn_setup():
        import jax, jax.numpy as jnp
        import numpy as np
        import math
        B, T, E, H = (2, 512, 256, 16)
        D = E // H
        key = jax.random.key(seed)
        ks = jax.random.split(key, 8)
        s = 1.0 / math.sqrt(E)
        return {'input': jax.random.normal(ks[0], (B, T, E), jnp.float32), 'encoded_features': jax.random.normal(ks[1], (B, T, E), jnp.float32), 'Wq': jax.random.normal(ks[2], (E, E), jnp.float32) * s, 'bq': jnp.zeros((E,), jnp.float32), 'Wkv': jax.random.normal(ks[3], (E, 2 * E), jnp.float32) * s, 'bkv': jnp.zeros((2 * E,), jnp.float32), 'Wo': jax.random.normal(ks[4], (E, E), jnp.float32) * s, 'bo': jnp.zeros((E,), jnp.float32)}
    _L0_xattn_all = _L0_xattn_setup()
    _L0_xattn_in = {k: v for k, v in _L0_xattn_all.items() if k in ('Wq', 'bq', 'Wkv', 'bkv', 'Wo', 'bo')}
    del _L0_xattn_all

    def _L0_ffn_setup():
        import jax, jax.numpy as jnp
        import numpy as np
        D_MODEL = 256
        D_FF = 1024
        N_EXPERTS = 8
        TOP_K = 2

        def _ffn(x, w1, b1, w2, b2):
            h = jax.nn.gelu(x @ w1.T + b1)
            return h @ w2.T + b2
        key = jax.random.key(seed)
        ks = jax.random.split(key, 12)
        s = 0.02
        x = jax.random.normal(ks[0], (4, 512, D_MODEL), dtype=jnp.float32)
        shared_w1 = jax.random.normal(ks[1], (D_FF, D_MODEL), dtype=jnp.float32) * s
        shared_b1 = jnp.zeros((D_FF,), dtype=jnp.float32)
        shared_w2 = jax.random.normal(ks[2], (D_MODEL, D_FF), dtype=jnp.float32) * s
        shared_b2 = jnp.zeros((D_MODEL,), dtype=jnp.float32)
        router_w = jax.random.normal(ks[3], (N_EXPERTS, D_MODEL), dtype=jnp.float32) * s
        router_b = jnp.zeros((N_EXPERTS,), dtype=jnp.float32)
        spec_w1 = jax.random.normal(ks[4], (N_EXPERTS, D_FF, D_MODEL), dtype=jnp.float32) * s
        spec_b1 = jnp.zeros((N_EXPERTS, D_FF), dtype=jnp.float32)
        spec_w2 = jax.random.normal(ks[5], (N_EXPERTS, D_MODEL, D_FF), dtype=jnp.float32) * s
        spec_b2 = jnp.zeros((N_EXPERTS, D_MODEL), dtype=jnp.float32)
        return dict(x=x, shared_w1=shared_w1, shared_b1=shared_b1, shared_w2=shared_w2, shared_b2=shared_b2, router_w=router_w, router_b=router_b, spec_w1=spec_w1, spec_b1=spec_b1, spec_w2=spec_w2, spec_b2=spec_b2)
    _L0_ffn_all = _L0_ffn_setup()
    _L0_ffn_in = {k: v for k, v in _L0_ffn_all.items() if k in ('shared_w1', 'shared_b1', 'shared_w2', 'shared_b2', 'router_w', 'router_b', 'spec_w1', 'spec_b1', 'spec_w2', 'spec_b2')}
    del _L0_ffn_all
    return {'x': x, 'ctx_1024': ctx_1024, 'g_xattn': g_xattn, 'g_ffn': g_ffn, 'L0_xattn_Wq': _L0_xattn_in['Wq'], 'L0_xattn_bq': _L0_xattn_in['bq'], 'L0_xattn_Wkv': _L0_xattn_in['Wkv'], 'L0_xattn_bkv': _L0_xattn_in['bkv'], 'L0_xattn_Wo': _L0_xattn_in['Wo'], 'L0_xattn_bo': _L0_xattn_in['bo'], 'L0_ffn_shared_w1': _L0_ffn_in['shared_w1'], 'L0_ffn_shared_b1': _L0_ffn_in['shared_b1'], 'L0_ffn_shared_w2': _L0_ffn_in['shared_w2'], 'L0_ffn_shared_b2': _L0_ffn_in['shared_b2'], 'L0_ffn_router_w': _L0_ffn_in['router_w'], 'L0_ffn_router_b': _L0_ffn_in['router_b'], 'L0_ffn_spec_w1': _L0_ffn_in['spec_w1'], 'L0_ffn_spec_b1': _L0_ffn_in['spec_b1'], 'L0_ffn_spec_w2': _L0_ffn_in['spec_w2'], 'L0_ffn_spec_b2': _L0_ffn_in['spec_b2']}

def reference(x, ctx_1024, g_xattn, g_ffn, L0_xattn_Wq, L0_xattn_bq, L0_xattn_Wkv, L0_xattn_bkv, L0_xattn_Wo, L0_xattn_bo, L0_ffn_shared_w1, L0_ffn_shared_b1, L0_ffn_shared_w2, L0_ffn_shared_b2, L0_ffn_router_w, L0_ffn_router_b, L0_ffn_spec_w1, L0_ffn_spec_b1, L0_ffn_spec_w2, L0_ffn_spec_b2):
    import jax
    import jax.numpy as jnp

    def _L0_xattn_ref(input, encoded_features, Wq, bq, Wkv, bkv, Wo, bo):
        import jax, jax.numpy as jnp
        import numpy as np
        import math
        B, T, E, H = (2, 512, 256, 16)
        D = E // H
        b, tq, _ = input.shape
        tk = encoded_features.shape[1]
        q = (input @ Wq + bq).reshape(b, tq, H, D).transpose(0, 2, 1, 3)
        kv = (encoded_features @ Wkv + bkv).reshape(b, tk, 2, H, D).transpose(2, 0, 3, 1, 4)
        k, v = (kv[0], kv[1])
        scores = jnp.einsum('bhqd,bhkd->bhqk', q, k) / math.sqrt(D)
        attn = jax.nn.softmax(scores, axis=2)
        out = jnp.einsum('bhqk,bhkd->bhqd', attn, v)
        out = out.transpose(0, 2, 1, 3).reshape(b, tq, H * D)
        return out @ Wo + bo

    def _L0_ffn_ref(x, shared_w1, shared_b1, shared_w2, shared_b2, router_w, router_b, spec_w1, spec_b1, spec_w2, spec_b2):
        import jax, jax.numpy as jnp
        import numpy as np
        D_MODEL = 256
        D_FF = 1024
        N_EXPERTS = 8
        TOP_K = 2

        def _ffn(x, w1, b1, w2, b2):
            h = jax.nn.gelu(x @ w1.T + b1)
            return h @ w2.T + b2
        B, T, D = x.shape
        xf = x.reshape(-1, D)
        U = xf.shape[0]
        logits = xf @ router_w.T + router_b
        routing = jax.nn.softmax(logits, axis=-1)
        sel_w, sel_idx = jax.lax.top_k(routing, TOP_K)
        sel_w = sel_w / sel_w.sum(axis=-1, keepdims=True)
        comb = jnp.zeros_like(routing).at[jnp.arange(U)[:, None], sel_idx].set(sel_w)
        shared_out = _ffn(xf, shared_w1, shared_b1, shared_w2, shared_b2)

        def body(acc, params):
            w1, b1, w2, b2, we = params
            return (acc + we[:, None] * _ffn(xf, w1, b1, w2, b2), None)
        acc0 = jnp.zeros_like(shared_out)
        acc, _ = jax.lax.scan(body, acc0, (spec_w1, spec_b1, spec_w2, spec_b2, comb.T))
        return (shared_out + acc).reshape(B, T, D)
    x = x + jnp.tanh(g_xattn[0]) * _L0_xattn_ref(_layernorm(x, axis=-1), ctx_1024, L0_xattn_Wq, L0_xattn_bq, L0_xattn_Wkv, L0_xattn_bkv, L0_xattn_Wo, L0_xattn_bo)
    x = x + jnp.tanh(g_ffn[0]) * _L0_ffn_ref(_layernorm(x, axis=-1), L0_ffn_shared_w1, L0_ffn_shared_b1, L0_ffn_shared_w2, L0_ffn_shared_b2, L0_ffn_router_w, L0_ffn_router_b, L0_ffn_spec_w1, L0_ffn_spec_b1, L0_ffn_spec_w2, L0_ffn_spec_b2)
    return x

_drawn_inputs = setup_inputs


def setup_inputs(seed=0):
    import zlib

    import numpy as np

    out = dict(_drawn_inputs(seed))
    spreads = {'L0_xattn_bq': (0.0, 0.8),
     'L0_xattn_bkv': (0.0, 0.1),
     'L0_xattn_bo': (0.0, 0.1),
     'L0_ffn_shared_b1': (0.0, 0.504),
     'L0_ffn_shared_b2': (0.0, 0.1),
     'L0_ffn_router_b': (0.0, 0.329),
     'L0_ffn_spec_b1': (0.0, 0.637),
     'L0_ffn_spec_b2': (0.0, 0.1)}
    factors = {}
    for name, (base, spread) in spreads.items():
        noise = np.random.default_rng([zlib.crc32(name.encode()), seed]).standard_normal(out[name].shape)
        drawn = base * np.exp(spread * noise) if base else spread * noise
        out[name] = jnp.asarray(drawn.astype(out[name].dtype))
    for name, factor in factors.items():
        out[name] = (out[name] * factor).astype(out[name].dtype)
    return out
```

```python
from contextlib import ExitStack

import concourse.bass as bass
from concourse import mybir

F32 = mybir.dt.float32
BF16 = mybir.dt.bfloat16
I32 = mybir.dt.int32
ALU = mybir.AluOpType
ACT = mybir.ActivationFunctionType
AX = mybir.AxisListType

P = 128
B, TQ, E = 16, 112, 256
TK, H, D = 375, 16, 16
EC = E // P
G, HG = 2, 8
KT, KR = 3, 125
UNITS = G * KT
NE, FF = 8, 1024
FC = FF // P
SHARED = NE
WE = EC * FF + FC * E
TOP = 2
TILES = (B * TQ * TOP) // P + NE - 1
SLOTS = TILES * P
CH = 2 * TQ
EPS = 1e-5
RING = 4
BIAS_STEPS = 10


def const_layout():
    at, out = 0, {}
    for name, width in (("ident", P), ("headmask", HG), ("parmask", 2), ("lower", TQ), ("expert", NE),
                        ("below", NE * NE), ("tile", TILES), ("sel", NE)):
        out[name] = (at, width)
        at += width
    return out, at


CONST, CONST_W = const_layout()


def build(nc, x, ctxT, wq, wkv, wo, bq, bk, bv, bo, gates, w, b1, b2, ws, b1s, b2s, rw, rb, consts, out):
    slots_d = nc.dram_tensor("slots_d", [SLOTS, E], F32).ap()
    y_d = nc.dram_tensor("y_d", [SLOTS, E], F32).ap()
    xn2_d = nc.dram_tensor("xn2_d", [B, TQ, E], F32).ap()

    with ExitStack() as ctx:
        def sb(name, shape, dt=F32):
            return ctx.enter_context(nc.sbuf_tensor(name, shape, dt))

        def ps(name, shape):
            return ctx.enter_context(nc.psum_tensor(name, shape, F32))

        def sem(name):
            return ctx.enter_context(nc.semaphore(name))

        W = sb("W", [P, NE + 1, WE])
        xall = sb("xall", [TQ, B, E])
        xn2T = sb("xn2T", [P, EC, B * TQ])
        cst = sb("cst", [P, CONST_W])
        sel = sb("sel", [P, NE, P], BF16)
        bparts = sb("bparts", [P, FF + E], BF16)
        small = sb("small", [P, 64])
        work = sb("work", [P, 6144])

        def const(name, rows=P):
            at, width = CONST[name]
            return cst[0:rows, at:at + width]

        ident = const("ident")

        class Region:

            def __init__(self, whole):
                self.whole, self.at = whole, 0

            def take(self, rows, *dims):
                n = 1
                for d in dims:
                    n *= d
                v = self.whole[0:rows, self.at:self.at + n]
                self.at += n
                assert self.at <= self.whole.shape[1]
                if len(dims) == 2:
                    return v.rearrange("p (a b) -> p a b", a=dims[0])
                if len(dims) == 3:
                    return v.rearrange("p (a b c) -> p a b c", a=dims[0], b=dims[1])
                return v

        late = Region(W[:, NE // 2:NE, :].rearrange("p e n -> p (e n)"))
        wq_s = late.take(P, EC, E)
        wkv_s = late.take(P, EC, 2 * E)
        wo_s = late.take(P, EC, E)
        ctx_s = [late.take(P, EC, TK) for _ in range(2)]
        kT = [late.take(P, G, TK) for _ in range(2)]
        V = [late.take(KR, KT, E) for _ in range(2)]
        qbd = [late.take(P, G, HG, TQ) for _ in range(2)]
        prob = [late.take(KR, HG, TQ) for _ in range(RING)]
        bias_rows = xn2T[:, 1, B * TQ - FF - E:]
        bias_part = xn2T[:, 0, B * TQ - (FF + E) // 2:].bitcast(BF16)
        zeros = xn2T[:, 0, B * TQ - (FF + E) // 2 - E:B * TQ - (FF + E) // 2]
        qs = [late.take(P, G, TQ) for _ in range(2)]
        otmp = late.take(P, G, TQ)
        oT = late.take(P, G, TQ)
        early = Region(work[:, 0:FC * CH * 2])
        xn = [early.take(TQ, E) for _ in range(2)]
        xn2 = [early.take(TQ, E) for _ in range(2)]
        x2 = [early.take(TQ, E) for _ in range(2)]
        xnT = early.take(P, EC, TQ)
        vs = [early.take(KR, P) for _ in range(RING)]
        bvb = early.take(KR, E)
        bob = early.take(TQ, E)
        b2b = early.take(TQ, E)
        mx = [early.take(KR, HG) for _ in range(2)]
        zz = [early.take(KR, HG) for _ in range(2)]
        rz = [early.take(KR, HG) for _ in range(2)]
        st1, mv1 = early.take(TQ, B, 6), early.take(TQ, B, 2)
        ve1, rstd1 = early.take(TQ, B), early.take(TQ, B)
        st2, mv2 = early.take(TQ, 6), early.take(TQ, 2)
        ve2, rstd2 = early.take(TQ, 1), early.take(TQ, 1)

        hT = [work[:, k * FC * CH:(k + 1) * FC * CH] for k in range(2)]
        hTs = [v.rearrange("p (f t) -> p f t", f=FC) for v in hT]
        hTe = [v[:, 0:FF].rearrange("p (f t) -> p f t", f=FC) for v in hT]
        ys = [v[:, FF:FF + E] for v in hT]
        xT = [v[:, FF + E:FF + 2 * E].rearrange("p (c t) -> p c t", c=EC) for v in hT]
        tail = Region(work[:, 2 * FC * CH:])
        xg = [tail.take(P, E) for _ in range(2)]
        h = [tail.take(P, FF) for _ in range(2)]
        stage = [xg[0][0:TQ], xg[1][0:TQ], h[1][0:TQ, 512:768], h[1][0:TQ, 768:1024]]
        scratch = Region(work[:, 2 * FC * CH + 2 * E:2 * FC * CH + 2 * E + FF + 512])
        bne = lambda: scratch.take(TQ, B, NE)
        lg, pr, oh1, oh2, t1, t2 = bne(), bne(), bne(), bne(), bne(), bne()
        hits = scratch.take(TQ, B * NE // 2).bitcast(BF16)
        lower_b = scratch.take(TQ, TQ // 2).bitcast(BF16)
        ones_b = scratch.take(TQ, TQ // 2).bitcast(BF16)
        bv_ = lambda: scratch.take(TQ, B)
        lmax, lsum, p1, p2, i1, i2 = bv_(), bv_(), bv_(), bv_(), bv_(), bv_()
        cnt, end, base = scratch.take(TQ, NE), scratch.take(TQ, NE), scratch.take(TQ, NE)
        cnt_i = scratch.take(TQ, NE).bitcast(I32)
        prod = scratch.take(TQ, NE, NE)
        teq, tef = scratch.take(1, TILES, NE - 1), scratch.take(1, TILES)
        slot_f = scratch.take(TQ, B, TOP)
        cw = sb("cw", [TQ, TOP, B])
        slot_i = sb("slot_i", [TQ, B, TOP], I32)
        tile_e = sb("tile_e", [1, TILES], I32)
        done = Region(W[:, 0:2, :].rearrange("p e n -> p (e n)"))
        yg = [[done.take(TQ, E) for _ in range(TOP)] for _ in range(B)]

        bq_s, bk_s, b1s_s, bq4 = small[:, 0:2], small[:, 2:4], small[:, 4:12], small[:, 12:14]
        gate_in, tg = small[0:TQ, 14:16], small[0:TQ, 16:18]
        mhalf = small[0:TQ, 18:19]
        rbb = small[0:TQ, 20:28]
        rw_s = small[:, 28:44].rearrange("p (c e) -> p c e", c=EC)

        bank = ctx.enter_context(nc.psum_tensor("bank", [P, 8, 512], F32))
        S = [bank[0:KR, 2 * k:2 * k + 2, 0:4 * TQ] for k in range(2)]
        O = bank[:, 4, :]
        J = [bank[:, 5 + k, :] for k in range(3)]
        Hp = [bank[:, 2 * k:2 * k + 2, :] for k in range(2)]
        HTp = bank[:, 4:6, :]
        XTp, Yp = bank[:, 6, :], bank[:, 7, :]

        c_in, wkv_in, wq_in, wo_in = sem("c_in"), sem("wkv_in"), sem("wq_in"), sem("wo_in")
        x_in = [sem(f"x_in{k}") for k in range(4)]
        ctx_in = [sem("ctx_in0"), sem("ctx_in1")]
        w_in, ws_in = sem("w_in"), sem("ws_in")
        xn2_stored = [sem("xn2_stored0"), sem("xn2_stored1")]
        setup_dve, setup_pool, setup_act = sem("setup_dve"), sem("setup_pool"), sem("setup_act")
        bias_zero, bias_in, bias_step = sem("bias_zero"), sem("bias_in"), sem("bias_step")
        zero_ready, slots_zeroed = sem("zero_ready"), sem("slots_zeroed")
        var1, rstd1_ready, xn_ready = sem("var1"), sem("rstd1_ready"), sem("xn_ready")
        xnT_ps, xnT_sb, q_ps, qs_sb, qbd_ready = sem("xnT_ps"), sem("xnT_sb"), sem("q_ps"), sem("qs_sb"), sem("qbd_ready")
        k_ps, k_sb, v_ps, v_sb = sem("k_ps"), sem("k_sb"), sem("v_ps"), sem("v_sb")
        qk_done, max_done, sub_done, exp_done = sem("qk_done"), sem("max_done"), sem("sub_done"), sem("exp_done")
        sum_done, rz_ready, vs_ready, pv_done = sem("sum_done"), sem("rz_ready"), sem("vs_ready"), sem("pv_done")
        otmp_ready, oT_ready, op_ps, x2_ready = sem("otmp_ready"), sem("oT_ready"), sem("op_ps"), sem("x2_ready")
        xbo_ready, b2_added = sem("xbo_ready"), sem("b2_added")
        st2_ready, mv2_ready, ve2_ready, rstd2_ready = sem("st2_ready"), sem("mv2_ready"), sem("ve2_ready"), sem("rstd2_ready")
        xn2_ready, xn2T_ps, xn2T_sb = sem("xn2_ready"), sem("xn2T_ps"), sem("xn2T_sb")
        lg_ps, rt, rt_exp_in, rt_exp, hits_ready, ranks_ps = (sem("lg_ps"), sem("rt"), sem("rt_exp_in"), sem("rt_exp"),
                                                            sem("hits_ready"), sem("ranks_ps"))
        routed = sem("routed")
        staged, scattered = [sem(f"staged{k}") for k in range(4)], [sem(f"scattered{k}") for k in range(4)]
        l1s_ps, hTs_sb, l2s_ps, shared_done = sem("l1s_ps"), sem("hTs_sb"), sem("l2s_ps"), sem("shared_done")
        xg_in = [sem("xg_in0"), sem("xg_in1")]
        xT_ps, xT_sb, l1_ps, h_sb, t_ps, hT_sb, l2_ps, y_sb = (sem("xT_ps"), sem("xT_sb"), sem("l1_ps"), sem("h_sb"),
                                                              sem("t_ps"), sem("hT_sb"), sem("l2_ps"), sem("y_sb"))
        y_stored = [sem("y_stored0"), sem("y_stored1")]
        gathered = [sem(f"gathered{b}") for b in range(B)]
        comb1, comb2, out_stored = sem("comb1"), sem("comb2"), sem("out_stored")

        class Step:

            def __init__(self, half, par):
                self.half, self.par, self.b = half, par, half * 2 + par

            def has(self, lo, hi):
                return not isinstance(self.b, int) or lo <= self.b <= hi

            def halves(self, off):
                return self.half + (self.par + off) // 2

        def ring(par, u):
            return (UNITS * par + u) % RING

        def phase1(engine, step):
            for b in range(-1, 4):
                step(Step(b // 2, b % 2))
            with engine.Fori(2, B // 2 - 1) as half:
                for par in range(2):
                    step(Step(half, par))
            for b in range(B - 2, B + 2):
                step(Step(b // 2, b % 2))

        def tiles_loop(engine, tile_step):
            for k in range(2):
                tile_step(0, k)
            with engine.Fori(1, (TILES - 3) // 2) as half:
                for k in range(2):
                    tile_step(half, k)

        def wait(engine, s, value):
            if not isinstance(value, int) or value > 0:
                engine.wait_ge(s, value)

        block = ctx.enter_context(nc.Block())

        @block.sync
        def _(sp):
            sp.dma_start(cst[:, :], consts).then_inc(c_in, 16)
            sp.dma_start(wkv_s, wkv).then_inc(wkv_in, 16)
            sp.dma_start(ctx_s[0], ctxT[0]).then_inc(ctx_in[0], 16)
            for k in range(4):
                sp.dma_start(xall[:, 4 * k:4 * k + 4, :], x[4 * k:4 * k + 4].rearrange("b t e -> t b e")).then_inc(x_in[k], 16)
                if k == 0:
                    sp.dma_start(wq_s, wq).then_inc(wq_in, 16)
                    for dst, src in ((bq_s, bq), (bk_s, bk), (b1s_s, b1s), (rw_s, rw)):
                        sp.dma_start(dst, src).then_inc(c_in, 16)
                    for dst, src, rows in ((bvb, bv, KR), (bob, bo, TQ), (b2b, b2s, TQ), (rbb, rb, TQ), (gate_in, gates, TQ)):
                        sp.dma_start(dst, src.partition_broadcast(rows)).then_inc(c_in, 16)
            sp.dma_start(ctx_s[1], ctxT[1]).then_inc(ctx_in[1], 16)
            sp.dma_start(wo_s, wo).then_inc(wo_in, 16)
            sp.wait_ge(bias_zero, 1)
            for k in range(3):
                sp.dma_start(bias_rows[32 * k:32 * k + NE, 0:FF], b1).then_inc(bias_in, 16)
                sp.dma_start(bias_rows[32 * k:32 * k + NE, FF:FF + E], b2).then_inc(bias_in, 16)
            for k in range(4):
                sp.dma_start(W[:, SHARED, k * 1024:(k + 1) * 1024], ws[k]).then_inc(ws_in, 16)
            sp.wait_ge(zero_ready, 1)
            sp.dma_start(slots_d.rearrange("(t p) e -> p t e", p=P),
                         zeros.unsqueeze(1).to_broadcast([P, TILES, E])).then_inc(slots_zeroed, 16)
            pieces = W[:, :, :].rearrange("p e (q n) -> p (e q) n", q=4)

            def step(s):
                b = s.b
                if s.has(0, B - 3):
                    sp.wait_ge(v_ps, 2 * b + 2)
                    sp.dma_start(ctx_s[s.par], ctxT[bass.ds(b + 2, 1)].rearrange("a p c k -> (a p) c k")
                                 ).then_inc(ctx_in[s.par], 16)
                if s.has(-1, B - 2):
                    sp.dma_start(pieces[:, bass.ds(b + 1, 1), :], w[bass.ds(b + 1, 1)].rearrange("a p n -> p a n")
                                 ).then_inc(w_in, 16)
                if s.has(2, B + 1):
                    sp.wait_ge(xn2_ready, b - 1)
                    sp.dma_start(xn2_d[bass.ds(b - 2, 1)].rearrange("a t e -> (a t) e"), xn2[s.par]
                                 ).then_inc(xn2_stored[s.par], 16)

            phase1(sp, step)
            sp.wait_ge(op_ps, B)
            sp.wait_ge(bias_step, BIAS_STEPS)
            sp.wait_ge(slots_zeroed, 16)
            for k in range(16, 32):
                sp.dma_start(pieces[:, k, :], w[k]).then_inc(w_in, 16)
            for k in range(2):
                sp.wait_ge(xn2_stored[k], 16 * B // 2)
            for b in range(B):
                if b >= 4:
                    sp.wait_ge(scattered[b % 4], 32 * (b // 4))
                sp.dma_start(stage[b % 4], xn2_d[b]).then_inc(staged[b % 4], 16)

            for k in range(4):
                sp.wait_ge(scattered[k], 32 * (B // 4))

            def load_rows(i, par):
                sp.dma_start(xg[par], slots_d[bass.ds(i * P, P), :]).then_inc(xg_in[par], 16)

            def store_rows(i, par):
                sp.wait_ge(y_sb, i + 1)
                sp.dma_start(y_d[bass.ds(i * P, P), :], ys[par]).then_inc(y_stored[par], 16)

            load_rows(0, 0)
            load_rows(1, 1)
            for i in range(2, 5):
                sp.wait_ge(xT_ps, i - 1)
                load_rows(i, i % 2)
            with sp.Fori(1, (TILES - 3) // 2) as half:
                for par in range(2):
                    i = half * 2 + par
                    sp.wait_ge(xT_ps, i + 2)
                    load_rows(i + 3, 1 - par)
                    store_rows(i - 2, par)
            for i in range(TILES - 5, TILES):
                store_rows(i, i % 2)
            for b in range(0, B, 2):
                sp.wait_ge(comb2, b + 2)
                sp.dma_start(out[b:b + 2].rearrange("b t e -> t b e"), xall[:, b:b + 2, :]).then_inc(out_stored, 16)
            sp.wait_ge(out_stored, 16 * B // 2)

        @block.tensor
        def _(pe):
            mm = nc.tensor.matmul

            def scores(s, u):
                g, kt, n = u // KT, u % KT, 6 * s.b + u
                if u == 0:
                    pe.wait_ge(qbd_ready, s.b + 1)
                if kt == 0:
                    pe.wait_ge(k_sb, 2 * s.b + g + 1)
                if u % 2 == 0:
                    wait(pe, exp_done, n - 1)
                else:
                    wait(pe, sub_done, 3 * s.b + (u - 1) // 2)
                for a in range(2):
                    last = mm(S[u % 2][:, a, :], kT[s.par][:, g, kt * KR:(kt + 1) * KR],
                              qbd[s.par][:, g, 4 * a:4 * a + 4, :], start=True, stop=True)
                last.then_inc(qk_done, 1)

            def values(b, par, u):
                g, kt, n = u // KT, u % KT, 6 * b + u
                pe.wait_ge(exp_done, n + 1)
                pe.wait_ge(vs_ready, n + 1)
                if u == 0:
                    wait(pe, oT_ready, b)
                for j in range(4):
                    last = mm(O[32 * j:32 * j + 32, g * 2 * TQ:(g + 1) * 2 * TQ], vs[ring(par, u)][:, 32 * j:32 * j + 32],
                              prob[ring(par, u)][:, 2 * j:2 * j + 2, :], start=(kt == 0), stop=(kt == KT - 1),
                              tile_position=(0, 32 * j), skip_group_check=True)
                last.then_inc(pv_done, 1)

            def step(s):
                b, nxt, npar = s.b, s.b + 1, 1 - s.par
                attend, prep = s.has(0, B - 1), s.has(-1, B - 2)
                prev, prev2 = s.has(1, B), s.has(2, B + 1)
                if prev:
                    values(b - 1, npar, 3)
                if attend:
                    scores(s, 0)
                if prep:
                    pe.wait_ge(xn_ready, nxt + 1)
                    wait(pe, v_sb, 2 * b + 2)
                    for c in range(EC):
                        last = nc.tensor.transpose(J[1][:, c * TQ:(c + 1) * TQ], xn[npar][:, c * P:(c + 1) * P], ident[0:TQ, 0:TQ])
                    last.then_inc(xnT_ps, 1)
                if prev:
                    values(b - 1, npar, 4)
                if attend:
                    scores(s, 1)
                if prep:
                    pe.wait_ge(ctx_in[npar], (s.halves(1) + 1) * 16)
                    if isinstance(b, int) and b < 0:
                        pe.wait_ge(wkv_in, 16)
                    wait(pe, xn2T_sb, b - 2)
                    for g in range(G):
                        if g == 1:
                            wait(pe, v_sb, 2 * b + 1)
                        for c in range(EC):
                            last = mm(J[2 - 2 * g][:, 0:TK], wkv_s[:, c, g * P:(g + 1) * P], ctx_s[npar][:, c, :],
                                      start=(c == 0), stop=(c == EC - 1))
                        last.then_inc(k_ps, 1)
                if prev:
                    values(b - 1, npar, 5)
                if attend:
                    scores(s, 2)
                if prep:
                    if isinstance(b, int) and b < 0:
                        pe.wait_ge(wq_in, 16)
                    pe.wait_ge(xnT_sb, nxt + 1)
                    for g in range(G):
                        for c in range(EC):
                            last = mm(J[1][:, g * TQ:(g + 1) * TQ], wq_s[:, c, g * P:(g + 1) * P], xnT[:, c, :],
                                      start=(c == 0), stop=(c == EC - 1))
                    last.then_inc(q_ps, 1)
                if attend:
                    values(b, s.par, 0)
                    scores(s, 3)
                if prev:
                    pe.wait_ge(oT_ready, b)
                    if prep:
                        pe.wait_ge(k_sb, 2 * b + 3)
                    else:
                        wait(pe, xn2T_sb, b - 2)
                    if isinstance(b, int) and b == 1:
                        pe.wait_ge(wo_in, 16)
                    for g in range(G):
                        last = mm(J[2][0:TQ, 0:E], oT[:, g, :], wo_s[:, g, :], start=(g == 0), stop=(g == G - 1))
                    last.then_inc(op_ps, 1)
                if prep:
                    pe.wait_ge(k_sb, 2 * b + 4)
                    for kt in range(2):
                        for c in range(EC):
                            last = mm(J[0][0:KR, kt * E:(kt + 1) * E], ctx_s[npar][:, c, kt * KR:(kt + 1) * KR],
                                      wkv_s[:, c, E:2 * E], start=(c == 0), stop=(c == EC - 1))
                    last.then_inc(v_ps, 1)
                if attend:
                    values(b, s.par, 1)
                    scores(s, 4)
                if prep:
                    pe.wait_ge(qs_sb, b + 2)
                    for c in range(EC):
                        last = mm(J[1][0:KR, 0:E], ctx_s[npar][:, c, 2 * KR:3 * KR], wkv_s[:, c, E:2 * E],
                                  start=(c == 0), stop=(c == EC - 1))
                    last.then_inc(v_ps, 1)
                if attend:
                    values(b, s.par, 2)
                    scores(s, 5)
                if prev2:
                    pe.wait_ge(xn2_ready, b - 1)
                    if prev:
                        pe.wait_ge(x2_ready, b)
                    else:
                        pe.wait_ge(xn2T_sb, b - 2)
                    for c in range(EC):
                        last = nc.tensor.transpose(J[2][:, c * TQ:(c + 1) * TQ], xn2[s.par][:, c * P:(c + 1) * P], ident[0:TQ, 0:TQ])
                    last.then_inc(xn2T_ps, 1)

            pe.wait_ge(c_in, 160)
            phase1(pe, step)

            pe.wait_ge(xn2T_sb, B)
            for b in range(B):
                for c in range(EC):
                    last = mm(J[0][0:TQ, b * NE:(b + 1) * NE], xn2T[:, c, b * TQ:(b + 1) * TQ], rw_s[:, c, :],
                              start=(c == 0), stop=(c == EC - 1))
            last.then_inc(lg_ps, 1)

            def shared_hidden(ch, n, par):
                for f in range(FC):
                    if f % 2 == 0:
                        wait(pe, hTs_sb, FC * n - FC + f + 2)
                    for c in range(EC):
                        last = mm(bank[:, f // 2, (f % 2) * CH:(f % 2 + 1) * CH],
                                  W[:, SHARED, c * FF + f * P:c * FF + (f + 1) * P],
                                  xn2T[:, c, bass.ds(ch * CH, CH)], start=(c == 0), stop=(c == EC - 1))
                    if f % 2 == 1:
                        last.then_inc(l1s_ps, 1)

            def shared_out(n, par):
                pe.wait_ge(hTs_sb, FC * n + FC)
                wait(pe, shared_done, 2 * n)
                for k in range(2):
                    for f in range(FC):
                        last = mm(HTp[0:TQ, k, 0:E], hTs[par][:, f, k * TQ:(k + 1) * TQ],
                                  W[:, SHARED, EC * FF + f * E:EC * FF + (f + 1) * E], start=(f == 0), stop=(f == FC - 1))
                    last.then_inc(l2s_ps, 1)

            pe.wait_ge(ws_in, 64)
            def ranks():
                pe.wait_ge(hits_ready, 1)
                R = XTp[0:TQ, 0:(B + 1) * NE]
                mm(R[:, 0:B * NE], lower_b, hits, start=True, stop=False, skip_group_check=True)
                for b in range(B):
                    last = mm(R[:, (b + 1) * NE:].rearrange("t (b e) -> t b e", e=NE), ones_b,
                              hits[:, b * NE:(b + 1) * NE].unsqueeze(1).to_broadcast([TQ, B - b, NE]),
                              start=False, stop=(b == B - 1), skip_group_check=True)
                last.then_inc(ranks_ps, 1)
            for par in range(2):
                shared_hidden(par, par, par)
            ranks()
            for par in range(2):
                shared_out(par, par)
            for par in range(2):
                shared_hidden(2 + par, 2 + par, par)
            for par in range(2):
                shared_out(2 + par, par)

            def turn_rows(i, par):
                wait(pe, xT_sb, i)
                for c in range(EC):
                    last = nc.tensor.transpose(XTp[:, c * P:(c + 1) * P], xg[par][:, c * P:(c + 1) * P], ident)
                last.then_inc(xT_ps, 1)

            def hidden(i, par):
                e = nc.tensor.value_load(tile_e[0:1, bass.ds(i, 1)], min_val=0, max_val=NE - 1)
                pe.wait_ge(xT_sb, i + 1)
                wait(pe, h_sb, i - 1)
                for a in range(2):
                    cols = slice(a * 512, (a + 1) * 512)
                    mm(Hp[par][:, a, :], sel[:, bass.ds(e, 1), :].rearrange("p a t -> p (a t)"), bparts[:, cols], start=True, stop=False)
                    for c in range(EC):
                        last = mm(Hp[par][:, a, :], xT[par][:, c, :],
                                  W[:, bass.ds(e, 1), c * FF + a * 512:c * FF + (a + 1) * 512].rearrange("p a n -> p (a n)"),
                                  start=False, stop=(c == EC - 1))
                last.then_inc(l1_ps, 1)

            def turn_hidden(i, par):
                pe.wait_ge(h_sb, i + 1)
                for a in range(2):
                    wait(pe, hT_sb, 2 * i - 1 + a)
                    for f in range(4):
                        last = nc.tensor.transpose(HTp[:, a, f * P:(f + 1) * P], h[par][:, (4 * a + f) * P:(4 * a + f + 1) * P], ident)
                    last.then_inc(t_ps, 1)

            def result(i, par):
                e = nc.tensor.value_load(tile_e[0:1, bass.ds(i, 1)], min_val=0, max_val=NE - 1)
                wait(pe, y_sb, i)
                pe.wait_ge(hT_sb, 2 * i + 1)
                mm(Yp[:, 0:E], sel[:, bass.ds(e, 1), :].rearrange("p a t -> p (a t)"), bparts[:, FF:FF + E], start=True, stop=False)
                for f in range(FC):
                    if f == 4:
                        pe.wait_ge(hT_sb, 2 * i + 2)
                    last = mm(Yp[:, 0:E], hTe[par][:, f, :],
                              W[:, bass.ds(e, 1), EC * FF + f * E:EC * FF + (f + 1) * E].rearrange("p a n -> p (a n)"),
                              start=False, stop=(f == FC - 1))
                last.then_inc(l2_ps, 1)

            pe.wait_ge(w_in, 16 * 32)
            pe.wait_ge(bias_step, BIAS_STEPS)
            pe.wait_ge(xg_in[0], 16)
            pe.wait_ge(hTs_sb, 4 * FC)
            pe.wait_ge(shared_done, 8)
            turn_rows(0, 0)
            pe.wait_ge(xg_in[1], 16)
            turn_rows(1, 1)
            hidden(0, 0)
            pe.wait_ge(xg_in[0], 32)
            turn_rows(2, 0)
            hidden(1, 1)
            turn_hidden(0, 0)

            def tile_step(half, k):
                i, par = half * 2 + 1 + k, (1 + k) % 2
                pe.wait_ge(xg_in[par], (half + (k + 3) // 2 + 1) * 16)
                turn_rows(i + 2, par)
                hidden(i + 1, 1 - par)
                turn_hidden(i, par)
                result(i - 1, 1 - par)

            tiles_loop(pe, tile_step)
            i = TILES - 2
            hidden(i + 1, (i + 1) % 2)
            turn_hidden(i, i % 2)
            result(i - 1, (i - 1) % 2)
            turn_hidden(i + 1, (i + 1) % 2)
            result(i, i % 2)
            result(i + 1, (i + 1) % 2)
            with pe.Fori(2, 4) as pair:
                for par in range(2):
                    shared_hidden(pair * 2 + par, pair * 2 + par, par)
                for par in range(2):
                    shared_out(pair * 2 + par, par)

        @block.scalar
        def _(act):
            act.wait_ge(c_in, 160)
            nc.scalar.activation(tg, gate_in, ACT.Tanh).then_inc(setup_act, 1)
            nc.scalar.activation(bq4, bq_s, ACT.Copy, scale=1.0 / D ** 0.5).then_inc(setup_act, 1)
            act.wait_ge(setup_act, 2)

            def exps(s, u):
                n = 6 * s.b + u
                if u % 2 == 0:
                    wait(act, pv_done, n + 1 - RING)
                    act.wait_ge(max_done, n + 1)
                    for hh in range(HG):
                        last = nc.scalar.activation(prob[ring(s.par, u)][:, hh, :], S[0][:, hh // 4, (hh % 4) * TQ:(hh % 4 + 1) * TQ],
                                                    ACT.Exp, bias=mx[0][:, hh:hh + 1], accum_out=zz[0][:, hh:hh + 1])
                    last.then_inc(exp_done, 1)
                else:
                    act.wait_ge(sub_done, 3 * s.b + (u + 1) // 2)
                    nc.scalar.activation(prob[ring(s.par, u)], prob[ring(s.par, u)], ACT.Exp).then_inc(exp_done, 1)

            def step(s):
                b, nxt, npar = s.b, s.b + 1, 1 - s.par
                attend, prep, prev2 = s.has(0, B - 1), s.has(-1, B - 2), s.has(2, B + 1)
                if isinstance(b, int) and b == 3:
                    act.wait_ge(slots_zeroed, 16)
                for u in range(UNITS):
                    if u == 3 and prep:
                        act.wait_ge(q_ps, nxt + 1)
                        wait(act, qbd_ready, b)
                        for g in range(G):
                            last = nc.scalar.activation(qs[npar][:, g, :], J[1][:, g * TQ:(g + 1) * TQ], ACT.Identity,
                                                        bias=bq4[:, g:g + 1], scale=1.0 / D ** 0.5)
                        last.then_inc(qs_sb, 1)
                    if attend:
                        exps(s, u)
                    if u == 0 and prep:
                        act.wait_ge(xnT_ps, nxt + 1)
                        wait(act, q_ps, nxt)
                        nc.scalar.activation(xnT, J[1][:, 0:EC * TQ].rearrange("p (c t) -> p c t", c=EC), ACT.Copy
                                             ).then_inc(xnT_sb, 1)
                    if u in (1, 2) and prep:
                        g = u - 1
                        act.wait_ge(k_ps, 2 * nxt + g + 1)
                        nc.scalar.activation(kT[npar][:, g, :], J[2 - 2 * g][:, 0:TK], ACT.Identity, bias=bk_s[:, g:g + 1]
                                             ).then_inc(k_sb, 1)
                if prev2:
                    act.wait_ge(xn2T_ps, b - 1)
                    nc.scalar.activation(xn2T[:, :, bass.ds((b - 2) * TQ, TQ)],
                                         J[2][:, 0:EC * TQ].rearrange("p (c t) -> p c t", c=EC), ACT.Copy).then_inc(xn2T_sb, 1)

            phase1(act, step)
            act.wait_ge(rt_exp_in, 1)
            nc.scalar.activation(pr, lg, ACT.Exp).then_inc(rt_exp, 1)
            act.wait_ge(b2_added, B)
            for k in range(2):
                act.wait_ge(xn2_stored[k], 16 * B // 2)

            def shared_gelu(n, par):
                wait(act, l2s_ps, 2 * n - 2)
                for f in range(FC):
                    act.wait_ge(l1s_ps, 4 * n + f // 2 + 1)
                    nc.scalar.activation(hTs[par][:, f, :], bank[:, f // 2, (f % 2) * CH:(f % 2 + 1) * CH],
                                         ACT.Gelu_apprx_tanh, bias=b1s_s[:, f:f + 1]).then_inc(hTs_sb, 1)

            for n in range(4):
                shared_gelu(n, n % 2)

            def copy_rows(i, par):
                act.wait_ge(xT_ps, i + 1)
                wait(act, l1_ps, i - 1)
                nc.scalar.activation(xT[par], XTp[:, 0:EC * P].rearrange("p (c t) -> p c t", c=EC), ACT.Copy).then_inc(xT_sb, 1)

            def gelu(i, par):
                act.wait_ge(l1_ps, i + 1)
                wait(act, t_ps, 2 * i - 2)
                nc.scalar.activation(h[par].rearrange("p (a n) -> p a n", a=2), Hp[par], ACT.Gelu_apprx_tanh).then_inc(h_sb, 1)

            act.wait_ge(l2s_ps, 8)
            copy_rows(0, 0)
            copy_rows(1, 1)
            gelu(0, 0)
            copy_rows(2, 0)
            gelu(1, 1)

            def tile_step(half, k):
                i, par = half * 2 + 1 + k, (1 + k) % 2
                copy_rows(i + 2, par)
                gelu(i + 1, 1 - par)

            tiles_loop(act, tile_step)
            gelu(TILES - 1, (TILES - 1) % 2)
            act.wait_ge(l2_ps, TILES)
            act.wait_ge(y_stored[0], 16 * ((TILES + 1) // 2))
            act.wait_ge(y_stored[1], 16 * (TILES // 2))
            with act.Fori(2, 4) as pair:
                for par in range(2):
                    shared_gelu(pair * 2 + par, par)

        @block.vector
        def _(dve):
            nc.vector.memset(mhalf, -0.5).then_inc(setup_dve, 1)
            nc.vector.memset(bias_rows, 0.0).then_inc(bias_zero, 1)
            nc.vector.memset(zeros, 0.0).then_inc(zero_ready, 1)
            for b in range(B):
                if b % 4 == 0:
                    dve.wait_ge(x_in[b // 4], 16)
                last = nc.vector.bn_stats(st1[:, b, :], xall[:, b, :])
            last.then_inc(var1, 1)
            dve.wait_ge(var1, 1)
            for b in range(B):
                last = nc.vector.bn_aggr(mv1[:, b, :], st1[:, b, :])
            last.then_inc(var1, 1)
            dve.wait_ge(var1, 2)
            nc.vector.tensor_scalar(ve1, mv1[:, :, 1], EPS, None, ALU.add).then_inc(var1, 1)
            dve.wait_ge(setup_act, 2)
            dve.wait_ge(c_in, 160)
            nc.vector.tensor_scalar(bob, bob, tg[:, 0:1], None, ALU.mult).then_inc(setup_dve, 1)
            nc.vector.tensor_scalar(b2b, b2b, tg[:, 1:2], None, ALU.mult).then_inc(setup_dve, 1)
            dve.wait_ge(rstd1_ready, 1)

            def normalise(b, par):
                nc.vector.tensor_scalar(xn[par], xall[:, bass.ds(b, 1), :].rearrange("t a e -> t (a e)"),
                                        mv1[:, bass.ds(b, 1), 0], rstd1[:, bass.ds(b, 1)], ALU.subtract, ALU.mult
                                        ).then_inc(xn_ready, 1)

            normalise(0, 0)
            normalise(1, 1)

            def maximum(s, u):
                dve.wait_ge(qk_done, 6 * s.b + u + 1)
                nc.vector.tensor_reduce(mx[u % 2].rearrange("k (a h) -> k a h", a=2), S[u % 2].rearrange("k a (h q) -> k a h q", q=TQ),
                                        AX.X, ALU.max, negate=(u % 2 == 0)).then_inc(max_done, 1)
                if u % 2:
                    n = 6 * s.b + u
                    dve.wait_ge(max_done, n + 1)
                    wait(dve, pv_done, n + 1 - RING)
                    nc.vector.tensor_tensor(prob[ring(s.par, u)].rearrange("k (a h) q -> k a h q", a=2), S[1].rearrange("k a (h q) -> k a h q", q=TQ),
                                            mx[1].rearrange("k (a h) -> k a h", a=2).unsqueeze(3).to_broadcast([KR, 2, 4, TQ]),
                                            ALU.subtract).then_inc(sub_done, 1)

            def one_over_sum(b, par, u):
                n = 6 * b + u
                dve.wait_ge(exp_done, n + 1)
                if u % 2:
                    nc.vector.tensor_reduce(zz[1], prob[ring(par, u)], AX.X, ALU.add).then_inc(sum_done, 1)
                    dve.wait_ge(sum_done, 3 * b + (u + 1) // 2)
                wait(dve, vs_ready, n - 1)
                nc.vector.reciprocal(rz[u % 2], zz[u % 2]).then_inc(rz_ready, 1)

            def step(s):
                b, nxt, npar = s.b, s.b + 1, 1 - s.par
                attend, prep = s.has(0, B - 1), s.has(-1, B - 2)
                prev, prev2 = s.has(1, B), s.has(2, B + 1)
                for u in range(UNITS):
                    if u == 2 and prev:
                        dve.wait_ge(pv_done, 6 * b)
                        wait(dve, op_ps, b - 1)
                        Ov = O[:, 0:G * 2 * TQ].rearrange("p (g r q) -> p g r q", g=G, r=2)
                        nc.vector.tensor_scalar(otmp, Ov[:, :, 0, :], const("parmask")[:, 0:1], None, ALU.mult).then_inc(otmp_ready, 1)
                        dve.wait_ge(otmp_ready, b)
                        nc.vector.scalar_tensor_tensor(oT, Ov[:, :, 1, :], const("parmask")[:, 1:2], otmp, ALU.mult, ALU.add
                                                       ).then_inc(oT_ready, 1)
                    if u == 5 and prev:
                        dve.wait_ge(st2_ready, b)
                    if attend:
                        maximum(s, u)
                    if u == 0 and prev:
                        one_over_sum(b - 1, npar, 5)
                    if u > 0 and attend:
                        one_over_sum(b, s.par, u - 1)
                    if u == 0 and s.has(0, B - 3):
                        dve.wait_ge(xnT_ps, b + 1)
                        normalise(b + 2, s.par)
                    if u == 0 and prev2:
                        dve.wait_ge(rstd2_ready, b - 1)
                        wait(dve, xn2_stored[s.par], (s.halves(-4) + 1) * 16)
                        nc.vector.tensor_scalar(xn2[s.par], x2[s.par], mv2[:, 0:1], rstd2, ALU.subtract, ALU.mult).then_inc(xn2_ready, 1)
                    if u == 4 and prev:
                        xb = xall[:, bass.ds(b - 1, 1), :].rearrange("t a e -> t (a e)")
                        dve.wait_ge(op_ps, b)
                        dve.wait_ge(xbo_ready, b)
                        wait(dve, b2_added, b - 2)
                        nc.vector.scalar_tensor_tensor(x2[npar], J[2][0:TQ, 0:E], tg[:, 0:1], xb, ALU.mult, ALU.add).then_inc(x2_ready, 1)
                        dve.wait_ge(x2_ready, b)
                        nc.vector.bn_stats(st2, x2[npar]).then_inc(st2_ready, 1)
                    if u == 4 and prep:
                        dve.wait_ge(v_ps, 2 * nxt + 1)
                        wait(dve, vs_ready, 6 * b)
                        nc.vector.tensor_tensor(V[npar][:, 0:2, :], J[0][0:KR, :].rearrange("k (a e) -> k a e", a=2),
                                                bvb.unsqueeze(1).to_broadcast([KR, 2, E]), ALU.add).then_inc(v_sb, 1)
                    if u == 5 and prev:
                        nc.vector.bn_aggr(mv2, st2).then_inc(mv2_ready, 1)
                        dve.wait_ge(mv2_ready, b)
                        nc.vector.tensor_scalar(ve2, mv2[:, 1:2], EPS, None, ALU.add).then_inc(ve2_ready, 1)
                    if u == 5 and prep:
                        dve.wait_ge(v_ps, 2 * nxt + 2)
                        nc.vector.tensor_tensor(V[npar][:, 2, :], J[1][0:KR, 0:E], bvb, ALU.add).then_inc(v_sb, 1)

            phase1(dve, step)

            steps = [0]

            def link(ins):
                steps[0] += 1
                ins.then_inc(rt, 1)
                dve.wait_ge(rt, steps[0])

            over_e = lambda v: v.unsqueeze(2).to_broadcast([TQ, B, NE])
            expert = const("expert", TQ).unsqueeze(1).to_broadcast([TQ, B, NE])
            dve.wait_ge(lg_ps, 1)
            link(nc.vector.tensor_tensor(lg, J[0][0:TQ, 0:B * NE].rearrange("t (b e) -> t b e", e=NE),
                                         rbb.unsqueeze(1).to_broadcast([TQ, B, NE]), ALU.add))
            link(nc.vector.tensor_reduce(lmax, lg, AX.X, ALU.max))
            nc.vector.tensor_tensor(lg, lg, over_e(lmax), ALU.subtract).then_inc(rt_exp_in, 1)
            link(nc.vector.memset(ones_b, 1.0))
            link(nc.vector.tensor_copy(lower_b, const("lower", TQ)))
            dve.wait_ge(rt_exp, 1)
            link(nc.vector.tensor_reduce(lsum, pr, AX.X, ALU.add))
            link(nc.vector.reciprocal(lsum, lsum))
            link(nc.vector.tensor_tensor(pr, pr, over_e(lsum), ALU.mult))

            def choose(p, i, oh):
                link(nc.vector.tensor_reduce(p, pr, AX.X, ALU.max))
                link(nc.vector.tensor_tensor(t1, pr, over_e(p), ALU.is_equal))
                link(nc.vector.tensor_tensor(t1, t1, expert, ALU.mult))
                link(nc.vector.tensor_reduce(i, t1, AX.X, ALU.min))
                link(nc.vector.tensor_tensor(oh, expert, over_e(i), ALU.is_equal))

            choose(p1, i1, oh1)
            link(nc.vector.scalar_tensor_tensor(pr, oh1, -2.0, pr, ALU.mult, ALU.add))
            choose(p2, i2, oh2)
            nc.vector.tensor_tensor(hits.rearrange("t (b e) -> t b e", e=NE), oh1, oh2, ALU.add).then_inc(hits_ready, 1)
            link(nc.vector.tensor_tensor(lsum, p1, p2, ALU.add))
            link(nc.vector.reciprocal(lsum, lsum))
            for k, p in enumerate((p1, p2)):
                link(nc.vector.scalar_tensor_tensor(cw[:, k, :], p, tg[:, 1:2], lsum, ALU.mult, ALU.mult))
            dve.wait_ge(ranks_ps, 1)
            ranks = XTp[0:TQ, 0:(B + 1) * NE].rearrange("t (b e) -> t b e", e=NE)
            link(nc.vector.tensor_scalar(cnt_i, ranks[:, B, :], float(P - 1), None, ALU.add))
            link(nc.vector.tensor_scalar(cnt_i, cnt_i, 7, None, ALU.arith_shift_right))
            link(nc.vector.tensor_copy(cnt, cnt_i))
            link(nc.vector.tensor_tensor(prod, const("below", TQ).rearrange("t (a b) -> t a b", a=NE),
                                         cnt.unsqueeze(1).to_broadcast([TQ, NE, NE]), ALU.mult))
            link(nc.vector.tensor_reduce(end, prod, AX.X, ALU.add))
            link(nc.vector.tensor_tensor(base, end, cnt, ALU.subtract))
            link(nc.vector.tensor_scalar(base, base, float(P), None, ALU.mult))
            link(nc.vector.tensor_tensor(t1, ranks[:, 0:B, :], base.unsqueeze(1).to_broadcast([TQ, B, NE]), ALU.add))
            for k, oh in enumerate((oh1, oh2)):
                link(nc.vector.tensor_tensor(t2, t1, oh, ALU.mult))
                link(nc.vector.tensor_reduce(slot_f[:, :, k], t2, AX.X, ALU.add))
            link(nc.vector.tensor_copy(slot_i[:, :, :], slot_f))
            link(nc.vector.tensor_tensor(teq, const("tile", 1).unsqueeze(2).to_broadcast([1, TILES, NE - 1]),
                                         end[0:1, 0:NE - 1].unsqueeze(1).to_broadcast([1, TILES, NE - 1]), ALU.is_ge))
            link(nc.vector.tensor_reduce(tef, teq, AX.X, ALU.add))
            nc.vector.tensor_copy(tile_e[:, :], tef).then_inc(routed, 1)

            def shared_add(n):
                for k in range(2):
                    b = 2 * n + k
                    dve.wait_ge(l2s_ps, b + 1)
                    dve.wait_ge(b2_added, b + 1)
                    nc.vector.scalar_tensor_tensor(xall[:, b, :], HTp[0:TQ, k, 0:E], tg[:, 1:2], xall[:, b, :], ALU.mult, ALU.add
                                                   ).then_inc(shared_done, 1)

            for n in range(4):
                shared_add(n)

            def copy_hidden(i, par):
                wait(dve, l2_ps, i - 1)
                for a in range(2):
                    dve.wait_ge(t_ps, 2 * i + a + 1)
                    nc.vector.tensor_copy(hTe[par][:, 4 * a:4 * a + 4, :], HTp[:, a, :].rearrange("p (f t) -> p f t", f=4)).then_inc(hT_sb, 1)

            def copy_result(i, half, par):
                dve.wait_ge(l2_ps, i + 1)
                wait(dve, y_stored[par], half * 16)
                nc.vector.tensor_copy(ys[par], Yp[:, 0:E]).then_inc(y_sb, 1)

            copy_hidden(0, 0)

            def tile_step(half, k):
                i, par = half * 2 + 1 + k, (1 + k) % 2
                copy_hidden(i, par)
                copy_result(i - 1, half, 1 - par)

            tiles_loop(dve, tile_step)
            for i in range(TILES - 2, TILES + 1):
                if i < TILES:
                    copy_hidden(i, i % 2)
                copy_result(i - 1, (i - 1) // 2, (i - 1) % 2)

            def combine(b):
                dve.wait_ge(gathered[b], 16 * TOP)
                dve.wait_ge(shared_done, b + 1)
                nc.vector.scalar_tensor_tensor(xall[:, b, :], yg[b][0], cw[:, 0, b:b + 1], xall[:, b, :], ALU.mult, ALU.add).then_inc(comb1, 1)
                dve.wait_ge(comb1, b + 1)
                nc.vector.scalar_tensor_tensor(xall[:, b, :], yg[b][1], cw[:, 1, b:b + 1], xall[:, b, :], ALU.mult, ALU.add).then_inc(comb2, 1)

            for n in range(4, 8):
                shared_add(n)
                for b in range(2 * (n - 4), 2 * (n - 4) + 2):
                    combine(b)
            for b in range(8, B):
                combine(b)

        @block.gpsimd
        def _(pool):
            pool.wait_ge(var1, 3)
            pool.wait_ge(setup_dve, 1)
            nc.gpsimd.tensor_tensor(rstd1, ve1, mhalf.to_broadcast([TQ, B]), ALU.pow).then_inc(rstd1_ready, 1)
            pool.wait_ge(c_in, 160)
            pool.wait_ge(setup_dve, 3)

            def scale_v(b, u, par):
                g, kt, n = u // KT, u % KT, 6 * b + u
                if kt == 0:
                    pool.wait_ge(v_sb, 2 * b + 2)
                wait(pool, pv_done, n + 1 - RING)
                pool.wait_ge(rz_ready, n + 1)
                nc.gpsimd.tensor_tensor(vs[ring(par, u)].rearrange("k (h d) -> k h d", h=HG), V[par][:, kt, g * P:(g + 1) * P].rearrange("k (h d) -> k h d", h=HG),
                                        rz[u % 2].unsqueeze(2).to_broadcast([KR, HG, D]), ALU.mult).then_inc(vs_ready, 1)

            def step(s):
                b, nxt, npar = s.b, s.b + 1, 1 - s.par
                attend, prep = s.has(0, B - 1), s.has(-1, B - 2)
                prev, prev2 = s.has(1, B), s.has(2, B + 1)
                if prev:
                    scale_v(b - 1, 5, npar)
                if attend:
                    scale_v(b, 0, s.par)
                    scale_v(b, 1, s.par)
                if prep:
                    xb = xall[:, bass.ds(nxt, 1), :].rearrange("t a e -> t (a e)")
                    pool.wait_ge(xn_ready, nxt + 1)
                    nc.gpsimd.tensor_tensor(xb, xb, bob, ALU.add).then_inc(xbo_ready, 1)
                if attend:
                    scale_v(b, 2, s.par)
                if prep:
                    pool.wait_ge(qs_sb, nxt + 1)
                    wait(pool, qk_done, 6 * b)
                    for g in range(G):
                        last = nc.gpsimd.tensor_tensor(qbd[npar][:, g, :, :], qs[npar][:, g, :].unsqueeze(1).to_broadcast([P, HG, TQ]),
                                                       const("headmask").unsqueeze(2).to_broadcast([P, HG, TQ]), ALU.mult)
                    last.then_inc(qbd_ready, 1)
                if attend:
                    scale_v(b, 3, s.par)
                if prev2:
                    xb = xall[:, bass.ds(b - 2, 1), :].rearrange("t a e -> t (a e)")
                    pool.wait_ge(xn2_ready, b - 1)
                    nc.gpsimd.tensor_tensor(xb, x2[s.par], b2b, ALU.add).then_inc(b2_added, 1)
                if attend:
                    scale_v(b, 4, s.par)
                if prev:
                    pool.wait_ge(ve2_ready, b)
                    wait(pool, xn2_ready, b - 1)
                    nc.gpsimd.tensor_tensor(rstd2, ve2, mhalf, ALU.pow).then_inc(rstd2_ready, 1)
                if isinstance(b, int) and b == 0:
                    bias_setup()
                if isinstance(b, int) and 1 <= b <= 3:
                    bias_split(b - 1)

            bias_steps = [0]

            def link(ins):
                bias_steps[0] += 1
                ins.then_inc(bias_step, 1)
                pool.wait_ge(bias_step, bias_steps[0])

            def bias_setup():
                link(nc.gpsimd.memset(bparts[:, :], 0.0))
                link(nc.gpsimd.tensor_copy(sel[:, :, :], const("sel").unsqueeze(2).to_broadcast([P, NE, P])))

            def bias_split(part):
                rows = slice(32 * part, 32 * part + 32)
                if part == 0:
                    pool.wait_ge(bias_in, 96)
                link(nc.gpsimd.tensor_copy(bias_part, bias_rows))
                link(nc.gpsimd.tensor_copy(bparts[rows, :], bias_part[rows]))
                if part < 2:
                    link(nc.gpsimd.tensor_tensor(bias_rows, bias_rows, bias_part, ALU.subtract))

            phase1(pool, step)
            pool.wait_ge(routed, 1)
            pool.wait_ge(slots_zeroed, 16)
            for b in range(B):
                pool.wait_ge(staged[b % 4], 16 * (b // 4 + 1))
                for k in range(TOP):
                    nc.gpsimd.indirect_dma_start(out=slots_d, out_offset=bass.IndirectOffsetOnAxis(ap=slot_i[:, b, k:k + 1], axis=0),
                                                 in_=stage[b % 4], in_offset=None).then_inc(scattered[b % 4], 16)
            pool.wait_ge(y_stored[0], 16 * ((TILES + 1) // 2))
            pool.wait_ge(y_stored[1], 16 * (TILES // 2))
            for b in range(B):
                for k in range(TOP):
                    nc.gpsimd.indirect_dma_start(out=yg[b][k], out_offset=None, in_=y_d,
                                                 in_offset=bass.IndirectOffsetOnAxis(ap=slot_i[:, b, k:k + 1], axis=0)).then_inc(gathered[b], 16)
    return nc


def _consts():
    import numpy as np

    c = np.zeros((P, CONST_W), np.float32)
    p = np.arange(P)[:, None]

    def put(name, v):
        at, width = CONST[name]
        c[:, at:at + width] = v

    put("ident", p == np.arange(P))
    put("headmask", p // D == np.arange(HG))
    put("parmask", (p // D) % 2 == np.arange(2))
    put("lower", p < np.arange(TQ))
    put("expert", np.arange(NE) - NE)
    put("below", (np.arange(NE) <= np.arange(NE)[:, None]).reshape(1, -1))
    put("tile", np.arange(TILES))
    put("sel", (p % 32 == np.arange(NE)) & (p < 96))
    return c


def _layout(inp):
    import numpy as np

    f = {k: np.asarray(v) for k, v in inp.items()}
    rows = lambda a: np.ascontiguousarray(a.reshape(-1, P, a.shape[-1]).transpose(1, 0, 2))
    col = lambda a: np.ascontiguousarray(a.reshape(-1, P).T)

    def experts(w1, w2):
        a = w1.transpose(0, 2, 1).reshape(-1, EC, P, FF).transpose(0, 2, 1, 3).reshape(-1, P, EC * FF)
        b = w2.transpose(0, 2, 1).reshape(-1, FC, P, E).transpose(0, 2, 1, 3).reshape(-1, P, FC * E)
        ab = np.concatenate([a, b], axis=2).reshape(-1, P, 4, WE // 4).transpose(0, 2, 1, 3)
        return np.ascontiguousarray(ab.reshape(-1, P, WE // 4))

    ctxT = f["ctx_1024"].transpose(0, 2, 1).reshape(B, EC, P, TK).transpose(0, 2, 1, 3)
    return {
        "x": f["x"], "ctxT": np.ascontiguousarray(ctxT),
        "wq": rows(f["L0_xattn_Wq"]), "wkv": rows(f["L0_xattn_Wkv"]), "wo": rows(f["L0_xattn_Wo"]),
        "bq": col(f["L0_xattn_bq"]), "bk": col(f["L0_xattn_bkv"][:E]), "bv": f["L0_xattn_bkv"][E:], "bo": f["L0_xattn_bo"],
        "gates": np.concatenate([f["g_xattn"], f["g_ffn"]]),
        "w": experts(f["L0_ffn_spec_w1"], f["L0_ffn_spec_w2"]), "b1": f["L0_ffn_spec_b1"], "b2": f["L0_ffn_spec_b2"],
        "ws": experts(f["L0_ffn_shared_w1"][None], f["L0_ffn_shared_w2"][None]), "b1s": col(f["L0_ffn_shared_b1"]), "b2s": f["L0_ffn_shared_b2"],
        "rw": rows(np.ascontiguousarray(f["L0_ffn_router_w"].T)), "rb": f["L0_ffn_router_b"],
        "consts": _consts(),
    }


def kernel(**inputs):
    import numpy as np
    import concourse.bacc as bacc
    from concourse.bass_utils import run_bass_kernel_spmd as run

    nc = bacc.Bacc("TRN2", target_bir_lowering=False, num_devices=1)
    arrays, args = {}, []
    for name, a in _layout(inputs).items():
        a = np.ascontiguousarray(a)
        arrays[f"in_{name}"] = a
        args.append(nc.dram_tensor(f"in_{name}", a.shape, mybir.dt.from_np(a.dtype), kind="ExternalInput").ap())
    args.append(nc.dram_tensor("out_0", (B, TQ, E), F32, kind="ExternalOutput").ap())
    build(nc, *args)
    r = run(nc, [arrays], core_ids=[0])
    return r.results[0]["out_0"]
```

```python
from contextlib import ExitStack

import concourse.bass as bass
from concourse import mybir

F32 = mybir.dt.float32
BF16 = mybir.dt.bfloat16
I32 = mybir.dt.int32
ALU = mybir.AluOpType
ACT = mybir.ActivationFunctionType
AX = mybir.AxisListType

P = 128
B, TQ, E = 16, 112, 256
TK, H, D = 375, 16, 16
EC = E // P
G, HG = 2, 8
KT, KR = 3, 125
UNITS = G * KT
NE, FF = 8, 1024
FC = FF // P
SHARED = NE
WE = EC * FF + FC * E
TOP = 2
TILES = (B * TQ * TOP) // P + NE - 1
SLOTS = TILES * P
CH = 2 * TQ
EPS = 1e-5
RING = 4


def const_layout():
    at, out = 0, {}
    for name, width in (("ident", P), ("headmask", HG), ("parmask", 2), ("lower", TQ), ("expert", NE),
                        ("below", NE * NE), ("tile", TILES), ("sel", NE)):
        out[name] = (at, width)
        at += width
    return out, at


CONST, CONST_W = const_layout()


def build(nc, x, ctxT, wq, wkv, wo, bq, bk, bv, bo, gates, w, b1, b2, ws, b1s, b2s, rw, rb, consts, out):
    slots_d = nc.dram_tensor("slots_d", [SLOTS, E], F32).ap()
    y_d = nc.dram_tensor("y_d", [SLOTS, E], F32).ap()
    xn2_d = nc.dram_tensor("xn2_d", [B, TQ, E], F32).ap()

    with ExitStack() as ctx:
        def sb(name, shape, dt=F32):
            return ctx.enter_context(nc.sbuf_tensor(name, shape, dt))

        def ps(name, shape):
            return ctx.enter_context(nc.psum_tensor(name, shape, F32))

        def sem(name):
            return ctx.enter_context(nc.semaphore(name))

        W = sb("W", [P, NE + 1, WE])
        xall = sb("xall", [TQ, B, E])
        xn2T = sb("xn2T", [P, EC, B * TQ])
        cst = sb("cst", [P, CONST_W])
        sel = sb("sel", [P, NE, P], BF16)
        bparts = sb("bparts", [P, FF + E], BF16)
        small = sb("small", [P, 64])
        work = sb("work", [P, 6144])

        def const(name, rows=P):
            at, width = CONST[name]
            return cst[0:rows, at:at + width]

        ident = const("ident")

        class Region:

            def __init__(self, whole):
                self.whole, self.at = whole, 0

            def take(self, rows, *dims):
                n = 1
                for d in dims:
                    n *= d
                v = self.whole[0:rows, self.at:self.at + n]
                self.at += n
                assert self.at <= self.whole.shape[1]
                if len(dims) == 2:
                    return v.rearrange("p (a b) -> p a b", a=dims[0])
                if len(dims) == 3:
                    return v.rearrange("p (a b c) -> p a b c", a=dims[0], b=dims[1])
                return v

        late = Region(W[:, NE // 2:NE, :].rearrange("p e n -> p (e n)"))
        wq_s = late.take(P, EC, E)
        wkv_s = late.take(P, EC, 2 * E)
        wo_s = late.take(P, EC, E)
        ctx_at = late.at
        ctx_s = [late.take(P, EC, TK) for _ in range(2)]
        kT = [late.take(P, G, TK) for _ in range(2)]
        V = [late.take(KR, KT, E) for _ in range(2)]
        qbd = [late.take(P, G, HG, TQ) for _ in range(2)]
        prob = [late.take(KR, HG, TQ) for _ in range(RING)]
        qs = [late.take(P, G, TQ) for _ in range(2)]
        otmp = late.take(P, G, TQ)
        oT = late.take(P, G, TQ)
        zeros = late.take(P, E)
        bias_rows = late.whole[:, NE // 2 * WE - FF - E:]
        assert late.at <= NE // 2 * WE - FF - E
        early = Region(work[:, 0:FC * CH * 2])
        xn = [early.take(TQ, E) for _ in range(2)]
        xn2 = [early.take(TQ, E) for _ in range(2)]
        x2 = [early.take(TQ, E) for _ in range(2)]
        xnT = early.take(P, EC, TQ)
        vs = [early.take(KR, P) for _ in range(RING)]
        bvb = early.take(KR, E)
        bob = early.take(TQ, E)
        b2b = early.take(TQ, E)
        mx = [early.take(KR, HG) for _ in range(2)]
        zz = [early.take(KR, HG) for _ in range(2)]
        rz = [early.take(KR, HG) for _ in range(2)]
        st1, mv1 = early.take(TQ, B, 6), early.take(TQ, B, 2)
        ve1, rstd1 = early.take(TQ, B), early.take(TQ, B)
        st2, mv2 = early.take(TQ, 6), early.take(TQ, 2)
        ve2, rstd2 = early.take(TQ, 1), early.take(TQ, 1)

        hT = [work[:, k * FC * CH:(k + 1) * FC * CH] for k in range(2)]
        hTs = [v.rearrange("p (f t) -> p f t", f=FC) for v in hT]
        hTe = [v[:, 0:FF].rearrange("p (f t) -> p f t", f=FC) for v in hT]
        ys = [v[:, FF:FF + E] for v in hT]
        xT = [v[:, FF + E:FF + 2 * E].rearrange("p (c t) -> p c t", c=EC) for v in hT]
        tail = Region(work[:, 2 * FC * CH:])
        xg = [tail.take(P, E) for _ in range(2)]
        h = [tail.take(P, FF) for _ in range(2)]
        stage = [xg[0][0:TQ], xg[1][0:TQ], h[1][0:TQ, 512:768], h[1][0:TQ, 768:1024]]
        scratch = Region(work[:, 2 * FC * CH + 2 * E:2 * FC * CH + 2 * E + FF + 512])
        bne = lambda: scratch.take(TQ, B, NE)
        lg, pr, oh1, oh2, t1, t2 = bne(), bne(), bne(), bne(), bne(), bne()
        hits = scratch.take(TQ, B * NE // 2).bitcast(BF16)
        lower_b = scratch.take(TQ, TQ // 2).bitcast(BF16)
        ones_b = scratch.take(TQ, TQ // 2).bitcast(BF16)
        bv_ = lambda: scratch.take(TQ, B)
        lmax, lsum, p1, p2, i1, i2 = bv_(), bv_(), bv_(), bv_(), bv_(), bv_()
        cnt, end, base = scratch.take(TQ, NE), scratch.take(TQ, NE), scratch.take(TQ, NE)
        cnt_i = scratch.take(TQ, NE).bitcast(I32)
        prod = scratch.take(TQ, NE, NE)
        teq, tef = scratch.take(1, TILES, NE - 1), scratch.take(1, TILES)
        slot_f = scratch.take(TQ, B, TOP)
        bias_part = h[0][:, 0:(FF + E) // 2].bitcast(BF16)
        cw = sb("cw", [TQ, TOP, B])
        slot_i = sb("slot_i", [TQ, B, TOP], I32)
        tile_e = sb("tile_e", [1, TILES], I32)
        done = Region(W[:, 0:2, :].rearrange("p e n -> p (e n)"))
        yg = [[done.take(TQ, E) for _ in range(TOP)] for _ in range(B)]

        bq_s, bk_s, b1s_s, bq4 = small[:, 0:2], small[:, 2:4], small[:, 4:12], small[:, 12:14]
        gate_in, tg = small[0:TQ, 14:16], small[0:TQ, 16:18]
        mhalf = small[0:TQ, 18:19]
        rbb = small[0:TQ, 20:28]
        rw_s = small[:, 28:44].rearrange("p (c e) -> p c e", c=EC)

        bank = ctx.enter_context(nc.psum_tensor("bank", [P, 8, 512], F32))
        S = [bank[0:KR, 2 * k:2 * k + 2, 0:4 * TQ] for k in range(2)]
        O = bank[:, 4, :]
        J = [bank[:, 5 + k, :] for k in range(3)]
        Hp = [bank[:, 2 * k:2 * k + 2, :] for k in range(2)]
        HTp = bank[:, 4:6, :]
        XTp, Yp = bank[:, 6, :], bank[:, 7, :]

        in_ctx, in_xn = late.whole[:, ctx_at:ctx_at + 2 * EC * TK], work[:, 0:2 * E]
        LOGITS = [(4 * k, 4, in_ctx[0:NE, 4 * k * TQ:4 * (k + 1) * TQ], J[1 - k % 2]) for k in range(3)]
        LOGITS += [(B - 4, 3, in_xn[0:NE, 0:3 * TQ], bank[:, 0, :]), (B - 1, 1, in_xn[0:NE, 3 * TQ:4 * TQ], bank[:, 1, :])]

        cst_in, gates_in, small_in, wkv_in, wq_in, wo_in = sem("cst_in"), sem("gates_in"), sem("small_in"), sem("wkv_in"), sem("wq_in"), sem("wo_in")
        x_in = [sem(f"x_in{k}") for k in range(4)]
        ctx_in = [sem("ctx_in0"), sem("ctx_in1")]
        w_in, ws_in = sem("w_in"), sem("ws_in")
        xn2_stored = [sem("xn2_stored0"), sem("xn2_stored1")]
        setup_dve, setup_pool, setup_act = sem("setup_dve"), sem("setup_pool"), sem("setup_act")
        zeroed, bias_in, bias_setup, bias_step, biases_ready = (sem("zeroed"), sem("bias_in"), sem("bias_setup"), sem("bias_step"),
                                                              sem("biases_ready"))
        slots_zeroed, router_in = sem("slots_zeroed"), sem("router_in")
        var1, rstd1_ready, xn_ready = sem("var1"), sem("rstd1_ready"), sem("xn_ready")
        xnT_ps, xnT_sb, q_ps, qs_sb, qbd_ready = sem("xnT_ps"), sem("xnT_sb"), sem("q_ps"), sem("qs_sb"), sem("qbd_ready")
        k_ps, k_sb, v_ps, v_sb = sem("k_ps"), sem("k_sb"), sem("v_ps"), sem("v_sb")
        qk_done, max_done, sub_done, exp_done = sem("qk_done"), sem("max_done"), sem("sub_done"), sem("exp_done")
        sum_done, rz_ready, vs_ready, pv_done = sem("sum_done"), sem("rz_ready"), sem("vs_ready"), sem("pv_done")
        otmp_ready, oT_ready, op_ps, x2_ready = sem("otmp_ready"), sem("oT_ready"), sem("op_ps"), sem("x2_ready")
        xbo_ready, b2_added = sem("xbo_ready"), sem("b2_added")
        st2_ready, mv2_ready, ve2_ready, rstd2_ready = sem("st2_ready"), sem("mv2_ready"), sem("ve2_ready"), sem("rstd2_ready")
        xn2_ready, xn2T_ps, xn2T_sb = sem("xn2_ready"), sem("xn2T_ps"), sem("xn2T_sb")
        lgT_ps, lgT_sb, lg_ps, rt, rt_exp_in, rt_exp, hits_ready, ranks_ps = (sem("lgT_ps"), sem("lgT_sb"), sem("lg_ps"), sem("rt"), sem("rt_exp_in"), sem("rt_exp"),
                                                            sem("hits_ready"), sem("ranks_ps"))
        routed = sem("routed")
        staged, scattered = [sem(f"staged{k}") for k in range(4)], [sem(f"scattered{k}") for k in range(4)]
        l1s_ps, hTs_sb, l2s_ps, shared_done = sem("l1s_ps"), sem("hTs_sb"), sem("l2s_ps"), sem("shared_done")
        xg_in = [sem("xg_in0"), sem("xg_in1")]
        xT_ps, xT_sb, l1_ps, h_sb, t_ps, hT_sb, l2_ps, y_sb = (sem("xT_ps"), sem("xT_sb"), sem("l1_ps"), sem("h_sb"),
                                                              sem("t_ps"), sem("hT_sb"), sem("l2_ps"), sem("y_sb"))
        y_stored = [sem("y_stored0"), sem("y_stored1")]
        gathered = [sem(f"gathered{b}") for b in range(B)]
        comb1, comb2, out_stored = sem("comb1"), sem("comb2"), sem("out_stored")

        class Step:

            def __init__(self, half, par):
                self.half, self.par, self.b = half, par, half * 2 + par

            def has(self, lo, hi):
                return not isinstance(self.b, int) or lo <= self.b <= hi

            def halves(self, off):
                return self.half + (self.par + off) // 2

        def ring(par, u):
            return (UNITS * par + u) % RING

        def phase1(engine, step):
            for b in range(-1, 4):
                step(Step(b // 2, b % 2))
            with engine.Fori(2, B // 2 - 1) as half:
                for par in range(2):
                    step(Step(half, par))
            for b in range(B - 2, B + 2):
                step(Step(b // 2, b % 2))

        def tiles_loop(engine, tile_step):
            for k in range(2):
                tile_step(0, k)
            with engine.Fori(1, (TILES - 3) // 2) as half:
                for k in range(2):
                    tile_step(half, k)

        def wait(engine, s, value):
            if not isinstance(value, int) or value > 0:
                engine.wait_ge(s, value)

        block = ctx.enter_context(nc.Block())

        @block.sync
        def _(sp):
            def load_x(k):
                sp.dma_start(xall[:, 4 * k:4 * k + 4, :], x[4 * k:4 * k + 4].rearrange("b t e -> t b e")).then_inc(x_in[k], 16)

            load_x(0)
            sp.dma_start(ctx_s[0], ctxT[0]).then_inc(ctx_in[0], 16)
            sp.dma_start(wkv_s, wkv).then_inc(wkv_in, 16)
            sp.dma_start(cst[:, :], consts).then_inc(cst_in, 16)
            sp.dma_start(wq_s, wq).then_inc(wq_in, 16)
            load_x(1)
            sp.dma_start(ctx_s[1], ctxT[1]).then_inc(ctx_in[1], 16)
            load_x(2)
            load_x(3)
            sp.dma_start(wo_s, wo).then_inc(wo_in, 16)
            for dst, src in ((b1s_s, b1s), (rw_s, rw), (rbb, rb.partition_broadcast(TQ))):
                sp.dma_start(dst, src).then_inc(router_in, 16)
            sp.wait_ge(zeroed, 2)
            for k in range(3):
                sp.dma_start(bias_rows[32 * k:32 * k + NE, 0:FF], b1).then_inc(bias_in, 16)
                sp.dma_start(bias_rows[32 * k:32 * k + NE, FF:FF + E], b2).then_inc(bias_in, 16)
            for k in range(4):
                sp.dma_start(W[:, SHARED, k * 1024:(k + 1) * 1024], ws[k]).then_inc(ws_in, 16)
            sp.dma_start(slots_d.rearrange("(t p) e -> p t e", p=P),
                         zeros.unsqueeze(1).to_broadcast([P, TILES, E])).then_inc(slots_zeroed, 16)
            pieces = W[:, :, :].rearrange("p e (q n) -> p (e q) n", q=4)

            def step(s):
                b = s.b
                if s.has(0, B - 3):
                    sp.wait_ge(v_ps, 2 * b + 2)
                    sp.dma_start(ctx_s[s.par], ctxT[bass.ds(b + 2, 1)].rearrange("a p c k -> (a p) c k")
                                 ).then_inc(ctx_in[s.par], 16)
                if s.has(-1, B - 2):
                    sp.dma_start(pieces[:, bass.ds(b + 1, 1), :], w[bass.ds(b + 1, 1)].rearrange("a p n -> p a n")
                                 ).then_inc(w_in, 16)
                if s.has(2, B + 1):
                    sp.wait_ge(xn2_ready, b - 1)
                    sp.dma_start(xn2_d[bass.ds(b - 2, 1)].rearrange("a t e -> (a t) e"), xn2[s.par]
                                 ).then_inc(xn2_stored[s.par], 16)

            phase1(sp, step)

            def stage_rows(b):
                if b >= 4:
                    sp.wait_ge(scattered[b % 4], 32 * (b // 4))
                sp.dma_start(stage[b % 4], xn2_d[b]).then_inc(staged[b % 4], 16)

            for k in range(2):
                sp.wait_ge(xn2_stored[k], 16 * (B // 2 - 1))
            for b in range(4):
                stage_rows(b)
            sp.wait_ge(op_ps, B)
            sp.wait_ge(lg_ps, 3)
            sp.wait_ge(slots_zeroed, 16)
            for k in range(16, 30):
                sp.dma_start(pieces[:, k, :], w[k]).then_inc(w_in, 16)
            for k in range(2):
                sp.wait_ge(xn2_stored[k], 16 * B // 2)
            for b in range(4, B):
                if b == 11:
                    sp.wait_ge(biases_ready, 1)
                    for k in range(30, 32):
                        sp.dma_start(pieces[:, k, :], w[k]).then_inc(w_in, 16)
                stage_rows(b)

            for k in range(4):
                sp.wait_ge(scattered[k], 32 * (B // 4))

            def load_rows(i, par):
                sp.dma_start(xg[par], slots_d[bass.ds(i * P, P), :]).then_inc(xg_in[par], 16)

            def store_rows(i, par):
                sp.wait_ge(y_sb, i + 1)
                sp.dma_start(y_d[bass.ds(i * P, P), :], ys[par]).then_inc(y_stored[par], 16)

            load_rows(0, 0)
            load_rows(1, 1)
            for i in range(2, 5):
                sp.wait_ge(xT_ps, i - 1)
                load_rows(i, i % 2)
            with sp.Fori(1, (TILES - 3) // 2) as half:
                for par in range(2):
                    i = half * 2 + par
                    sp.wait_ge(xT_ps, i + 2)
                    load_rows(i + 3, 1 - par)
                    store_rows(i - 2, par)
            for i in range(TILES - 5, TILES):
                store_rows(i, i % 2)
            for b in range(0, B, 2):
                sp.wait_ge(comb2, b + 2)
                sp.dma_start(out[b:b + 2].rearrange("b t e -> t b e"), xall[:, b:b + 2, :]).then_inc(out_stored, 16)
            sp.wait_ge(out_stored, 16 * B // 2)

        @block.tensor
        def _(pe):
            mm = nc.tensor.matmul

            def scores(s, u):
                g, kt, n = u // KT, u % KT, 6 * s.b + u
                if kt == 0:
                    pe.wait_ge(qbd_ready, 2 * s.b + g + 1)
                    pe.wait_ge(k_sb, 2 * s.b + g + 1)
                if u % 2 == 0:
                    wait(pe, exp_done, n - 1)
                else:
                    wait(pe, sub_done, 3 * s.b + (u - 1) // 2)
                for a in range(2):
                    last = mm(S[u % 2][:, a, :], kT[s.par][:, g, kt * KR:(kt + 1) * KR],
                              qbd[s.par][:, g, 4 * a:4 * a + 4, :], start=True, stop=True)
                last.then_inc(qk_done, 1)

            def values(b, par, u):
                g, kt, n = u // KT, u % KT, 6 * b + u
                pe.wait_ge(exp_done, n + 1)
                pe.wait_ge(vs_ready, n + 1)
                if u == 0:
                    wait(pe, oT_ready, b)
                for j in range(4):
                    last = mm(O[32 * j:32 * j + 32, g * 2 * TQ:(g + 1) * 2 * TQ], vs[ring(par, u)][:, 32 * j:32 * j + 32],
                              prob[ring(par, u)][:, 2 * j:2 * j + 2, :], start=(kt == 0), stop=(kt == KT - 1),
                              tile_position=(0, 32 * j), skip_group_check=True)
                last.then_inc(pv_done, 1)

            def logits(k):
                first, n, _, at = LOGITS[k]
                if k == 2:
                    pe.wait_ge(lgT_sb, 1)
                for c in range(EC):
                    last = mm(at[0:NE, 0:n * TQ], rw_s[:, c, :], xn2T[:, c, first * TQ:(first + n) * TQ],
                              start=(c == 0), stop=(c == EC - 1))
                last.then_inc(lgT_ps, 1)

            def turn_logits(k):
                first, n, rows, _ = LOGITS[k]
                pe.wait_ge(lgT_sb, max(k, 2) + 1)
                for b in range(n):
                    last = nc.tensor.transpose(J[1][0:TQ, (first + b) * NE:(first + b + 1) * NE], rows[:, b * TQ:(b + 1) * TQ], ident[0:NE, 0:NE])
                last.then_inc(lg_ps, 1)

            def turn_x(s):
                b, nxt, npar = s.b, s.b + 1, 1 - s.par
                pe.wait_ge(xn_ready, nxt + 1)
                if isinstance(b, int) and b < 0:
                    pe.wait_ge(cst_in, 16)
                wait(pe, v_sb, 2 * b + 2)
                for c in range(EC):
                    last = nc.tensor.transpose(J[1][:, c * TQ:(c + 1) * TQ], xn[npar][:, c * P:(c + 1) * P], ident[0:TQ, 0:TQ])
                last.then_inc(xnT_ps, 1)

            def project_k(s, groups=range(G)):
                b, nxt, npar = s.b, s.b + 1, 1 - s.par
                pe.wait_ge(ctx_in[npar], (s.halves(1) + 1) * 16)
                if isinstance(b, int) and b < 0:
                    pe.wait_ge(wkv_in, 16)
                for g in groups:
                    if g == 0:
                        wait(pe, v_sb, 2 * b + 1)
                    else:
                        wait(pe, xn2T_sb, b - 2)
                    for c in range(EC):
                        last = mm(J[2 * g][:, 0:TK], wkv_s[:, c, g * P:(g + 1) * P], ctx_s[npar][:, c, :],
                                  start=(c == 0), stop=(c == EC - 1))
                    last.then_inc(k_ps, 1)

            def step(s):
                b, nxt, npar = s.b, s.b + 1, 1 - s.par
                attend, prep = s.has(0, B - 1), s.has(-1, B - 2)
                prev, prev2 = s.has(1, B), s.has(2, B + 1)
                first = isinstance(b, int) and b < 0
                if attend:
                    scores(s, 0)
                if first:
                    project_k(s, (0,))
                if prep:
                    turn_x(s)
                if first:
                    project_k(s, (1,))
                if prev:
                    values(b - 1, npar, 3)
                if attend:
                    scores(s, 1)
                if prep and not first:
                    project_k(s)
                if isinstance(b, int) and b == B - 1:
                    pe.wait_ge(v_sb, 2 * B)
                    pe.wait_ge(xn2T_sb, 12)
                    pe.wait_ge(router_in, 48)
                    logits(0)
                if isinstance(b, int) and b == B:
                    logits(2)
                if prev:
                    values(b - 1, npar, 4)
                if prev:
                    values(b - 1, npar, 5)
                if attend:
                    scores(s, 2)
                if prep:
                    if isinstance(b, int) and b < 0:
                        pe.wait_ge(wq_in, 16)
                    pe.wait_ge(xnT_sb, nxt + 1)
                    for g in range(G):
                        for c in range(EC):
                            last = mm(J[1][:, g * TQ:(g + 1) * TQ], wq_s[:, c, g * P:(g + 1) * P], xnT[:, c, :],
                                      start=(c == 0), stop=(c == EC - 1))
                    last.then_inc(q_ps, 1)
                if prep:
                    pe.wait_ge(k_sb, 2 * b + 3)
                    for kt in range(2):
                        for c in range(EC):
                            last = mm(J[0][0:KR, kt * E:(kt + 1) * E], ctx_s[npar][:, c, kt * KR:(kt + 1) * KR],
                                      wkv_s[:, c, E:2 * E], start=(c == 0), stop=(c == EC - 1))
                    last.then_inc(v_ps, 1)
                if attend:
                    values(b, s.par, 0)
                    scores(s, 3)
                if isinstance(b, int) and b == B - 1:
                    logits(1)
                if attend:
                    values(b, s.par, 1)
                    scores(s, 4)
                if prev:
                    pe.wait_ge(oT_ready, b)
                    if prep:
                        pe.wait_ge(k_sb, 2 * b + 4)
                    else:
                        wait(pe, xn2T_sb, b - 2)
                    if isinstance(b, int) and b == 1:
                        pe.wait_ge(wo_in, 16)
                    for g in range(G):
                        last = mm(J[2][0:TQ, 0:E], oT[:, g, :], wo_s[:, g, :], start=(g == 0), stop=(g == G - 1))
                    last.then_inc(op_ps, 1)
                if isinstance(b, int) and b == B:
                    for k in range(3):
                        turn_logits(k)
                if isinstance(b, int) and b == B + 1:
                    pe.wait_ge(xn2T_sb, B - 1)
                    logits(3)
                if prep:
                    pe.wait_ge(qs_sb, b + 2)
                    for c in range(EC):
                        last = mm(J[1][0:KR, 0:E], ctx_s[npar][:, c, 2 * KR:3 * KR], wkv_s[:, c, E:2 * E],
                                  start=(c == 0), stop=(c == EC - 1))
                    last.then_inc(v_ps, 1)
                if attend:
                    values(b, s.par, 2)
                    scores(s, 5)
                if prev2:
                    pe.wait_ge(xn2_ready, b - 1)
                    if prev:
                        pe.wait_ge(x2_ready, b)
                    else:
                        pe.wait_ge(xn2T_sb, b - 2)
                    for c in range(EC):
                        last = nc.tensor.transpose(J[2][:, c * TQ:(c + 1) * TQ], xn2[s.par][:, c * P:(c + 1) * P], ident[0:TQ, 0:TQ])
                    last.then_inc(xn2T_ps, 1)

            phase1(pe, step)

            pe.wait_ge(xn2T_sb, B)
            logits(4)
            turn_logits(3)
            turn_logits(4)

            def shared_hidden(ch, n, par):
                for f in range(FC):
                    if f % 2 == 0:
                        wait(pe, hTs_sb, FC * n - FC + f + 2)
                    for c in range(EC):
                        last = mm(bank[:, f // 2, (f % 2) * CH:(f % 2 + 1) * CH],
                                  W[:, SHARED, c * FF + f * P:c * FF + (f + 1) * P],
                                  xn2T[:, c, bass.ds(ch * CH, CH)], start=(c == 0), stop=(c == EC - 1))
                    if f % 2 == 1:
                        last.then_inc(l1s_ps, 1)

            def shared_out(n, par):
                pe.wait_ge(hTs_sb, FC * n + FC)
                for k in range(2):
                    wait(pe, shared_done, 2 * n - 1 + k)
                    for f in range(FC):
                        last = mm(HTp[0:TQ, k, 0:E], hTs[par][:, f, k * TQ:(k + 1) * TQ],
                                  W[:, SHARED, EC * FF + f * E:EC * FF + (f + 1) * E], start=(f == 0), stop=(f == FC - 1))
                    last.then_inc(l2s_ps, 1)

            pe.wait_ge(ws_in, 64)
            def ranks():
                pe.wait_ge(hits_ready, 1)
                R = XTp[0:TQ, 0:(B + 1) * NE]
                mm(R[:, 0:B * NE], lower_b, hits, start=True, stop=False, skip_group_check=True)
                for b in range(B):
                    last = mm(R[:, (b + 1) * NE:].rearrange("t (b e) -> t b e", e=NE), ones_b,
                              hits[:, b * NE:(b + 1) * NE].unsqueeze(1).to_broadcast([TQ, B - b, NE]),
                              start=False, stop=(b == B - 1), skip_group_check=True)
                last.then_inc(ranks_ps, 1)
            shared_hidden(0, 0, 0)
            ranks()
            shared_hidden(1, 1, 1)
            for par in range(2):
                shared_out(par, par)
            for par in range(2):
                shared_hidden(2 + par, 2 + par, par)
            for par in range(2):
                shared_out(2 + par, par)

            def turn_rows(i, par):
                wait(pe, xT_sb, i)
                for c in range(EC):
                    last = nc.tensor.transpose(XTp[:, c * P:(c + 1) * P], xg[par][:, c * P:(c + 1) * P], ident)
                last.then_inc(xT_ps, 1)

            def hidden(i, par):
                e = nc.tensor.value_load(tile_e[0:1, bass.ds(i, 1)], min_val=0, max_val=NE - 1)
                pe.wait_ge(xT_sb, i + 1)
                wait(pe, h_sb, i - 1)
                for a in range(2):
                    cols = slice(a * 512, (a + 1) * 512)
                    mm(Hp[par][:, a, :], sel[:, bass.ds(e, 1), :].rearrange("p a t -> p (a t)"), bparts[:, cols], start=True, stop=False)
                    for c in range(EC):
                        last = mm(Hp[par][:, a, :], xT[par][:, c, :],
                                  W[:, bass.ds(e, 1), c * FF + a * 512:c * FF + (a + 1) * 512].rearrange("p a n -> p (a n)"),
                                  start=False, stop=(c == EC - 1))
                last.then_inc(l1_ps, 1)

            def turn_hidden(i, par):
                pe.wait_ge(h_sb, i + 1)
                for a in range(2):
                    wait(pe, hT_sb, 2 * i - 1 + a)
                    for f in range(4):
                        last = nc.tensor.transpose(HTp[:, a, f * P:(f + 1) * P], h[par][:, (4 * a + f) * P:(4 * a + f + 1) * P], ident)
                    last.then_inc(t_ps, 1)

            def result(i, par):
                e = nc.tensor.value_load(tile_e[0:1, bass.ds(i, 1)], min_val=0, max_val=NE - 1)
                wait(pe, y_sb, i)
                pe.wait_ge(hT_sb, 2 * i + 1)
                mm(Yp[:, 0:E], sel[:, bass.ds(e, 1), :].rearrange("p a t -> p (a t)"), bparts[:, FF:FF + E], start=True, stop=False)
                for f in range(FC):
                    if f == 4:
                        pe.wait_ge(hT_sb, 2 * i + 2)
                    last = mm(Yp[:, 0:E], hTe[par][:, f, :],
                              W[:, bass.ds(e, 1), EC * FF + f * E:EC * FF + (f + 1) * E].rearrange("p a n -> p (a n)"),
                              start=False, stop=(f == FC - 1))
                last.then_inc(l2_ps, 1)

            pe.wait_ge(w_in, 16 * 32)
            pe.wait_ge(biases_ready, 1)
            pe.wait_ge(xg_in[0], 16)
            pe.wait_ge(hTs_sb, 4 * FC)
            pe.wait_ge(shared_done, 8)
            turn_rows(0, 0)
            pe.wait_ge(xg_in[1], 16)
            turn_rows(1, 1)
            hidden(0, 0)
            pe.wait_ge(xg_in[0], 32)
            turn_rows(2, 0)
            hidden(1, 1)
            turn_hidden(0, 0)

            def tile_step(half, k):
                i, par = half * 2 + 1 + k, (1 + k) % 2
                pe.wait_ge(xg_in[par], (half + (k + 3) // 2 + 1) * 16)
                turn_rows(i + 2, par)
                hidden(i + 1, 1 - par)
                turn_hidden(i, par)
                result(i - 1, 1 - par)

            tiles_loop(pe, tile_step)
            i = TILES - 2
            hidden(i + 1, (i + 1) % 2)
            turn_hidden(i, i % 2)
            result(i - 1, (i - 1) % 2)
            turn_hidden(i + 1, (i + 1) % 2)
            result(i, i % 2)
            result(i + 1, (i + 1) % 2)
            with pe.Fori(2, 4) as pair:
                for par in range(2):
                    shared_hidden(pair * 2 + par, pair * 2 + par, par)
                for par in range(2):
                    shared_out(pair * 2 + par, par)

        @block.scalar
        def _(act):
            for dst, src in ((gate_in, gates.partition_broadcast(TQ)), (bq_s, bq), (bk_s, bk)):
                act.dma_start(dst, src).then_inc(gates_in, 16)
            for dst, src in ((bob, bo.partition_broadcast(TQ)), (b2b, b2s.partition_broadcast(TQ)), (bvb, bv.partition_broadcast(KR))):
                act.dma_start(dst, src).then_inc(small_in, 16)
            act.wait_ge(gates_in, 16 * 3)
            nc.scalar.activation(tg, gate_in, ACT.Tanh).then_inc(setup_act, 1)
            nc.scalar.activation(bq4, bq_s, ACT.Copy, scale=1.0 / D ** 0.5).then_inc(setup_act, 1)
            act.wait_ge(setup_act, 2)

            def copy_logits(k):
                act.wait_ge(lgT_ps, k + 1)
                nc.scalar.activation(LOGITS[k][2], LOGITS[k][3][0:NE, 0:LOGITS[k][1] * TQ], ACT.Copy).then_inc(lgT_sb, 1)

            def exps(s, u):
                n = 6 * s.b + u
                if u % 2 == 0:
                    wait(act, pv_done, n + 1 - RING)
                    act.wait_ge(max_done, n + 1)
                    for hh in range(HG):
                        last = nc.scalar.activation(prob[ring(s.par, u)][:, hh, :], S[0][:, hh // 4, (hh % 4) * TQ:(hh % 4 + 1) * TQ],
                                                    ACT.Exp, bias=mx[0][:, hh:hh + 1], accum_out=zz[0][:, hh:hh + 1])
                    last.then_inc(exp_done, 1)
                else:
                    act.wait_ge(sub_done, 3 * s.b + (u + 1) // 2)
                    nc.scalar.activation(prob[ring(s.par, u)], prob[ring(s.par, u)], ACT.Exp).then_inc(exp_done, 1)

            def step(s):
                b, nxt, npar = s.b, s.b + 1, 1 - s.par
                attend, prep, prev2 = s.has(0, B - 1), s.has(-1, B - 2), s.has(2, B + 1)
                for u in range(UNITS):
                    if u == 2 and prep:
                        act.wait_ge(q_ps, nxt + 1)
                        wait(act, qbd_ready, 2 * b)
                        for g in range(G):
                            last = nc.scalar.activation(qs[npar][:, g, :], J[1][:, g * TQ:(g + 1) * TQ], ACT.Identity,
                                                        bias=bq4[:, g:g + 1], scale=1.0 / D ** 0.5)
                        last.then_inc(qs_sb, 1)
                    if attend:
                        exps(s, u)
                    if u in (2, 4) and isinstance(b, int) and b == B - 1:
                        copy_logits(u // 2 - 1)
                    if u == 0 and prep:
                        act.wait_ge(xnT_ps, nxt + 1)
                        wait(act, q_ps, nxt)
                        nc.scalar.activation(xnT, J[1][:, 0:EC * TQ].rearrange("p (c t) -> p c t", c=EC), ACT.Copy
                                             ).then_inc(xnT_sb, 1)
                    if u == 1 and prep:
                        for g in range(G):
                            act.wait_ge(k_ps, 2 * nxt + g + 1)
                            nc.scalar.activation(kT[npar][:, g, :], J[2 * g][:, 0:TK], ACT.Identity, bias=bk_s[:, g:g + 1]
                                                 ).then_inc(k_sb, 1)
                if isinstance(b, int) and b == B:
                    copy_logits(2)
                if isinstance(b, int) and b == B + 1:
                    copy_logits(3)
                if prev2:
                    act.wait_ge(xn2T_ps, b - 1)
                    nc.scalar.activation(xn2T[:, :, bass.ds((b - 2) * TQ, TQ)],
                                         J[2][:, 0:EC * TQ].rearrange("p (c t) -> p c t", c=EC), ACT.Copy).then_inc(xn2T_sb, 1)

            phase1(act, step)
            copy_logits(4)
            act.wait_ge(rt_exp_in, 1)
            nc.scalar.activation(pr, lg, ACT.Exp).then_inc(rt_exp, 1)
            act.wait_ge(b2_added, B)
            for k in range(2):
                act.wait_ge(xn2_stored[k], 16 * B // 2)

            def shared_gelu(n, par):
                wait(act, l2s_ps, 2 * n - 2)
                for f in range(FC):
                    act.wait_ge(l1s_ps, 4 * n + f // 2 + 1)
                    nc.scalar.activation(hTs[par][:, f, :], bank[:, f // 2, (f % 2) * CH:(f % 2 + 1) * CH],
                                         ACT.Gelu_apprx_tanh, bias=b1s_s[:, f:f + 1]).then_inc(hTs_sb, 1)

            for n in range(4):
                shared_gelu(n, n % 2)

            def copy_rows(i, par):
                act.wait_ge(xT_ps, i + 1)
                wait(act, l1_ps, i - 1)
                nc.scalar.activation(xT[par], XTp[:, 0:EC * P].rearrange("p (c t) -> p c t", c=EC), ACT.Copy).then_inc(xT_sb, 1)

            def gelu(i, par):
                act.wait_ge(l1_ps, i + 1)
                wait(act, t_ps, 2 * i - 2)
                nc.scalar.activation(h[par].rearrange("p (a n) -> p a n", a=2), Hp[par], ACT.Gelu_apprx_tanh).then_inc(h_sb, 1)

            act.wait_ge(l2s_ps, 8)
            copy_rows(0, 0)
            copy_rows(1, 1)
            gelu(0, 0)
            copy_rows(2, 0)
            gelu(1, 1)

            def tile_step(half, k):
                i, par = half * 2 + 1 + k, (1 + k) % 2
                copy_rows(i + 2, par)
                gelu(i + 1, 1 - par)

            tiles_loop(act, tile_step)
            gelu(TILES - 1, (TILES - 1) % 2)
            act.wait_ge(l2_ps, TILES)
            act.wait_ge(y_stored[0], 16 * ((TILES + 1) // 2))
            act.wait_ge(y_stored[1], 16 * (TILES // 2))
            with act.Fori(2, 4) as pair:
                for par in range(2):
                    shared_gelu(pair * 2 + par, par)

        @block.vector
        def _(dve):
            nc.vector.memset(mhalf, -0.5).then_inc(setup_dve, 1)

            def statistics(k):
                dve.wait_ge(x_in[k], 16)
                for b in range(4 * k, 4 * k + 4):
                    last = nc.vector.bn_stats(st1[:, b, :], xall[:, b, :])
                last.then_inc(var1, 1)
                dve.wait_ge(var1, 3 * k + 1)
                for b in range(4 * k, 4 * k + 4):
                    last = nc.vector.bn_aggr(mv1[:, b, :], st1[:, b, :])
                last.then_inc(var1, 1)
                dve.wait_ge(var1, 3 * k + 2)
                nc.vector.tensor_scalar(ve1[:, 4 * k:4 * k + 4], mv1[:, 4 * k:4 * k + 4, 1], EPS, None, ALU.add).then_inc(var1, 1)

            def normalise(b, par):
                nc.vector.tensor_scalar(xn[par], xall[:, bass.ds(b, 1), :].rearrange("t a e -> t (a e)"),
                                        mv1[:, bass.ds(b, 1), 0], rstd1[:, bass.ds(b, 1)], ALU.subtract, ALU.mult
                                        ).then_inc(xn_ready, 1)

            statistics(0)
            dve.wait_ge(rstd1_ready, 1)
            normalise(0, 0)
            normalise(1, 1)
            dve.wait_ge(setup_act, 2)
            dve.wait_ge(small_in, 16 * 3)
            nc.vector.tensor_scalar(bob, bob, tg[:, 0:1], None, ALU.mult).then_inc(setup_dve, 1)
            nc.vector.tensor_scalar(b2b, b2b, tg[:, 1:2], None, ALU.mult).then_inc(setup_dve, 1)

            def maximum(s, u):
                dve.wait_ge(qk_done, 6 * s.b + u + 1)
                nc.vector.tensor_reduce(mx[u % 2].rearrange("k (a h) -> k a h", a=2), S[u % 2].rearrange("k a (h q) -> k a h q", q=TQ),
                                        AX.X, ALU.max, negate=(u % 2 == 0)).then_inc(max_done, 1)
                if u % 2:
                    n = 6 * s.b + u
                    dve.wait_ge(max_done, n + 1)
                    wait(dve, pv_done, n + 1 - RING)
                    nc.vector.tensor_tensor(prob[ring(s.par, u)].rearrange("k (a h) q -> k a h q", a=2), S[1].rearrange("k a (h q) -> k a h q", q=TQ),
                                            mx[1].rearrange("k (a h) -> k a h", a=2).unsqueeze(3).to_broadcast([KR, 2, 4, TQ]),
                                            ALU.subtract).then_inc(sub_done, 1)

            def one_over_sum(b, par, u):
                n = 6 * b + u
                dve.wait_ge(exp_done, n + 1)
                if u % 2:
                    nc.vector.tensor_reduce(zz[1], prob[ring(par, u)], AX.X, ALU.add).then_inc(sum_done, 1)
                    dve.wait_ge(sum_done, 3 * b + (u + 1) // 2)
                wait(dve, vs_ready, n - 1)
                nc.vector.reciprocal(rz[u % 2], zz[u % 2]).then_inc(rz_ready, 1)

            def step(s):
                b, nxt, npar = s.b, s.b + 1, 1 - s.par
                attend, prep = s.has(0, B - 1), s.has(-1, B - 2)
                prev, prev2 = s.has(1, B), s.has(2, B + 1)
                if isinstance(b, int) and b == 0:
                    dve.wait_ge(cst_in, 16)
                if isinstance(b, int) and b in (2, 3):
                    dve.wait_ge(rstd1_ready, 2 if b == 2 else 4)
                for u in range(UNITS):
                    if u == 2 and prev:
                        dve.wait_ge(pv_done, 6 * b)
                        wait(dve, op_ps, b - 1)
                        Ov = O[:, 0:G * 2 * TQ].rearrange("p (g r q) -> p g r q", g=G, r=2)
                        nc.vector.tensor_scalar(otmp, Ov[:, :, 0, :], const("parmask")[:, 0:1], None, ALU.mult).then_inc(otmp_ready, 1)
                        dve.wait_ge(otmp_ready, b)
                        nc.vector.scalar_tensor_tensor(oT, Ov[:, :, 1, :], const("parmask")[:, 1:2], otmp, ALU.mult, ALU.add
                                                       ).then_inc(oT_ready, 1)
                    if u == 5 and prev:
                        xb = xall[:, bass.ds(b - 1, 1), :].rearrange("t a e -> t (a e)")
                        dve.wait_ge(op_ps, b)
                        dve.wait_ge(xbo_ready, b)
                        wait(dve, b2_added, b - 2)
                        nc.vector.scalar_tensor_tensor(x2[npar], J[2][0:TQ, 0:E], tg[:, 0:1], xb, ALU.mult, ALU.add).then_inc(x2_ready, 1)
                    if u == 5 and prep:
                        dve.wait_ge(v_ps, 2 * nxt + 2)
                        nc.vector.tensor_tensor(V[npar][:, 2, :], J[1][0:KR, 0:E], bvb, ALU.add).then_inc(v_sb, 1)
                    if u == 5 and prev:
                        dve.wait_ge(x2_ready, b)
                        nc.vector.bn_stats(st2, x2[npar]).then_inc(st2_ready, 1)
                        dve.wait_ge(st2_ready, b)
                    if attend:
                        maximum(s, u)
                    if u == 5 and prev:
                        nc.vector.bn_aggr(mv2, st2).then_inc(mv2_ready, 1)
                    if u == 0 and prev:
                        one_over_sum(b - 1, npar, 5)
                    if u > 0 and attend:
                        one_over_sum(b, s.par, u - 1)
                    if u == 5 and prev:
                        dve.wait_ge(mv2_ready, b)
                        nc.vector.tensor_scalar(ve2, mv2[:, 1:2], EPS, None, ALU.add).then_inc(ve2_ready, 1)
                    if u == 2 and s.has(0, B - 3):
                        dve.wait_ge(xnT_ps, b + 1)
                        normalise(b + 2, s.par)
                    if u == 2 and prev2:
                        dve.wait_ge(rstd2_ready, b - 1)
                        wait(dve, xn2_stored[s.par], (s.halves(-4) + 1) * 16)
                        nc.vector.tensor_scalar(xn2[s.par], x2[s.par], mv2[:, 0:1], rstd2, ALU.subtract, ALU.mult).then_inc(xn2_ready, 1)
                    if u == 4 and prep:
                        dve.wait_ge(v_ps, 2 * nxt + 1)
                        wait(dve, vs_ready, 6 * b)
                        nc.vector.tensor_tensor(V[npar][:, 0:2, :], J[0][0:KR, :].rearrange("k (a e) -> k a e", a=2),
                                                bvb.unsqueeze(1).to_broadcast([KR, 2, E]), ALU.add).then_inc(v_sb, 1)
                if isinstance(b, int) and b < 2:
                    statistics(b + 2)

            phase1(dve, step)

            steps = [0]

            def link(ins):
                steps[0] += 1
                ins.then_inc(rt, 1)
                dve.wait_ge(rt, steps[0])

            over_e = lambda v: v.unsqueeze(2).to_broadcast([TQ, B, NE])
            expert = const("expert", TQ).unsqueeze(1).to_broadcast([TQ, B, NE])
            dve.wait_ge(lg_ps, len(LOGITS))
            link(nc.vector.tensor_tensor(lg, J[1][0:TQ, 0:B * NE].rearrange("t (b e) -> t b e", e=NE),
                                         rbb.unsqueeze(1).to_broadcast([TQ, B, NE]), ALU.add))
            link(nc.vector.tensor_reduce(lmax, lg, AX.X, ALU.max))
            nc.vector.tensor_tensor(lg, lg, over_e(lmax), ALU.subtract).then_inc(rt_exp_in, 1)
            link(nc.vector.memset(ones_b, 1.0))
            link(nc.vector.tensor_copy(lower_b, const("lower", TQ)))
            dve.wait_ge(rt_exp, 1)
            link(nc.vector.tensor_reduce(lsum, pr, AX.X, ALU.add))
            link(nc.vector.reciprocal(lsum, lsum))
            link(nc.vector.tensor_tensor(pr, pr, over_e(lsum), ALU.mult))

            def choose(p, i, oh):
                link(nc.vector.tensor_reduce(p, pr, AX.X, ALU.max))
                link(nc.vector.tensor_tensor(t1, pr, over_e(p), ALU.is_equal))
                link(nc.vector.tensor_tensor(t1, t1, expert, ALU.mult))
                link(nc.vector.tensor_reduce(i, t1, AX.X, ALU.min))
                link(nc.vector.tensor_tensor(oh, expert, over_e(i), ALU.is_equal))

            choose(p1, i1, oh1)
            link(nc.vector.scalar_tensor_tensor(pr, oh1, -2.0, pr, ALU.mult, ALU.add))
            choose(p2, i2, oh2)
            nc.vector.tensor_tensor(hits.rearrange("t (b e) -> t b e", e=NE), oh1, oh2, ALU.add).then_inc(hits_ready, 1)
            link(nc.vector.tensor_tensor(lsum, p1, p2, ALU.add))
            link(nc.vector.reciprocal(lsum, lsum))
            for k, p in enumerate((p1, p2)):
                link(nc.vector.scalar_tensor_tensor(cw[:, k, :], p, tg[:, 1:2], lsum, ALU.mult, ALU.mult))
            dve.wait_ge(ranks_ps, 1)
            ranks = XTp[0:TQ, 0:(B + 1) * NE].rearrange("t (b e) -> t b e", e=NE)
            link(nc.vector.tensor_scalar(cnt_i, ranks[:, B, :], float(P - 1), None, ALU.add))
            link(nc.vector.tensor_scalar(cnt_i, cnt_i, 7, None, ALU.arith_shift_right))
            link(nc.vector.tensor_copy(cnt, cnt_i))
            link(nc.vector.tensor_tensor(prod, const("below", TQ).rearrange("t (a b) -> t a b", a=NE),
                                         cnt.unsqueeze(1).to_broadcast([TQ, NE, NE]), ALU.mult))
            link(nc.vector.tensor_reduce(end, prod, AX.X, ALU.add))
            link(nc.vector.tensor_tensor(base, end, cnt, ALU.subtract))
            link(nc.vector.tensor_scalar(base, base, float(P), None, ALU.mult))
            link(nc.vector.tensor_tensor(t1, ranks[:, 0:B, :], base.unsqueeze(1).to_broadcast([TQ, B, NE]), ALU.add))
            for k, oh in enumerate((oh1, oh2)):
                link(nc.vector.tensor_tensor(t2, t1, oh, ALU.mult))
                link(nc.vector.tensor_reduce(slot_f[:, :, k], t2, AX.X, ALU.add))
            link(nc.vector.tensor_copy(slot_i[:, :, :], slot_f))
            link(nc.vector.tensor_tensor(teq, const("tile", 1).unsqueeze(2).to_broadcast([1, TILES, NE - 1]),
                                         end[0:1, 0:NE - 1].unsqueeze(1).to_broadcast([1, TILES, NE - 1]), ALU.is_ge))
            link(nc.vector.tensor_reduce(tef, teq, AX.X, ALU.add))
            nc.vector.tensor_copy(tile_e[:, :], tef).then_inc(routed, 1)

            def shared_add(n):
                for k in range(2):
                    b = 2 * n + k
                    dve.wait_ge(l2s_ps, b + 1)
                    dve.wait_ge(b2_added, b + 1)
                    nc.vector.scalar_tensor_tensor(xall[:, b, :], HTp[0:TQ, k, 0:E], tg[:, 1:2], xall[:, b, :], ALU.mult, ALU.add
                                                   ).then_inc(shared_done, 1)

            shared_add(0)
            parts = [0]

            def part_link(ins):
                parts[0] += 1
                ins.then_inc(bias_step, 1)
                dve.wait_ge(bias_step, parts[0])

            dve.wait_ge(routed, 1)
            dve.wait_ge(bias_in, 96)
            dve.wait_ge(bias_setup, 2)
            for part in range(3):
                rows = slice(32 * part, 32 * part + 32)
                part_link(nc.vector.tensor_copy(bias_part, bias_rows))
                last = nc.vector.tensor_copy(bparts[rows, :], bias_part[rows])
                if part < 2:
                    part_link(last)
                    part_link(nc.vector.tensor_tensor(bias_rows, bias_rows, bias_part, ALU.subtract))
            last.then_inc(biases_ready, 1)
            for n in range(1, 4):
                shared_add(n)

            def copy_hidden(i, par):
                wait(dve, l2_ps, i - 1)
                for a in range(2):
                    dve.wait_ge(t_ps, 2 * i + a + 1)
                    nc.vector.tensor_copy(hTe[par][:, 4 * a:4 * a + 4, :], HTp[:, a, :].rearrange("p (f t) -> p f t", f=4)).then_inc(hT_sb, 1)

            def copy_result(i, half, par):
                dve.wait_ge(l2_ps, i + 1)
                wait(dve, y_stored[par], half * 16)
                nc.vector.tensor_copy(ys[par], Yp[:, 0:E]).then_inc(y_sb, 1)

            copy_hidden(0, 0)

            def tile_step(half, k):
                i, par = half * 2 + 1 + k, (1 + k) % 2
                copy_hidden(i, par)
                copy_result(i - 1, half, 1 - par)

            tiles_loop(dve, tile_step)
            for i in range(TILES - 2, TILES + 1):
                if i < TILES:
                    copy_hidden(i, i % 2)
                copy_result(i - 1, (i - 1) // 2, (i - 1) % 2)

            def combine(b):
                dve.wait_ge(gathered[b], 16 * TOP)
                dve.wait_ge(shared_done, b + 1)
                nc.vector.scalar_tensor_tensor(xall[:, b, :], yg[b][0], cw[:, 0, b:b + 1], xall[:, b, :], ALU.mult, ALU.add).then_inc(comb1, 1)
                dve.wait_ge(comb1, b + 1)
                nc.vector.scalar_tensor_tensor(xall[:, b, :], yg[b][1], cw[:, 1, b:b + 1], xall[:, b, :], ALU.mult, ALU.add).then_inc(comb2, 1)

            shared_add(4)
            shared_add(5)
            for b in range(12):
                combine(b)
            for n in range(6, 8):
                shared_add(n)
                for b in range(2 * n, 2 * n + 2):
                    combine(b)

        @block.gpsimd
        def _(pool):
            nc.gpsimd.memset(bias_rows, 0.0).then_inc(zeroed, 1)
            nc.gpsimd.memset(zeros, 0.0).then_inc(zeroed, 1)
            pool.wait_ge(setup_dve, 1)

            def rstd_first(k):
                pool.wait_ge(var1, 3 * k + 3)
                nc.gpsimd.tensor_tensor(rstd1[:, 4 * k:4 * k + 4], ve1[:, 4 * k:4 * k + 4], mhalf.to_broadcast([TQ, 4]), ALU.pow
                                        ).then_inc(rstd1_ready, 1)

            rstd_first(0)
            pool.wait_ge(cst_in, 16)
            pool.wait_ge(setup_dve, 3)

            def scale_v(b, u, par):
                g, kt, n = u // KT, u % KT, 6 * b + u
                if kt == 0:
                    pool.wait_ge(v_sb, 2 * b + 2)
                wait(pool, pv_done, n + 1 - RING)
                pool.wait_ge(rz_ready, n + 1)
                nc.gpsimd.tensor_tensor(vs[ring(par, u)].rearrange("k (h d) -> k h d", h=HG), V[par][:, kt, g * P:(g + 1) * P].rearrange("k (h d) -> k h d", h=HG),
                                        rz[u % 2].unsqueeze(2).to_broadcast([KR, HG, D]), ALU.mult).then_inc(vs_ready, 1)

            def step(s):
                b, nxt, npar = s.b, s.b + 1, 1 - s.par
                attend, prep = s.has(0, B - 1), s.has(-1, B - 2)
                prev, prev2 = s.has(1, B), s.has(2, B + 1)
                if prev:
                    scale_v(b - 1, 5, npar)
                if attend:
                    scale_v(b, 0, s.par)
                    scale_v(b, 1, s.par)
                if prep:
                    xb = xall[:, bass.ds(nxt, 1), :].rearrange("t a e -> t (a e)")
                    pool.wait_ge(xn_ready, nxt + 1)
                    nc.gpsimd.tensor_tensor(xb, xb, bob, ALU.add).then_inc(xbo_ready, 1)
                if prep:
                    pool.wait_ge(qs_sb, nxt + 1)
                    wait(pool, qk_done, 6 * b)
                    for g in range(G):
                        nc.gpsimd.tensor_tensor(qbd[npar][:, g, :, :], qs[npar][:, g, :].unsqueeze(1).to_broadcast([P, HG, TQ]),
                                                       const("headmask").unsqueeze(2).to_broadcast([P, HG, TQ]), ALU.mult).then_inc(qbd_ready, 1)
                if attend:
                    scale_v(b, 2, s.par)
                    scale_v(b, 3, s.par)
                if prev2:
                    xb = xall[:, bass.ds(b - 2, 1), :].rearrange("t a e -> t (a e)")
                    pool.wait_ge(xn2_ready, b - 1)
                    nc.gpsimd.tensor_tensor(xb, x2[s.par], b2b, ALU.add).then_inc(b2_added, 1)
                if attend:
                    scale_v(b, 4, s.par)
                if prev:
                    pool.wait_ge(ve2_ready, b)
                    wait(pool, xn2_ready, b - 1)
                    nc.gpsimd.tensor_tensor(rstd2, ve2, mhalf, ALU.pow).then_inc(rstd2_ready, 1)
                if isinstance(b, int) and 0 <= b < 3:
                    rstd_first(b + 1)

            phase1(pool, step)
            nc.gpsimd.memset(bparts[:, :], 0.0).then_inc(bias_setup, 1)
            nc.gpsimd.tensor_copy(sel[:, :, :], const("sel").unsqueeze(2).to_broadcast([P, NE, P])).then_inc(bias_setup, 1)
            pool.wait_ge(routed, 1)
            pool.wait_ge(slots_zeroed, 16)
            for b in range(B):
                pool.wait_ge(staged[b % 4], 16 * (b // 4 + 1))
                for k in range(TOP):
                    nc.gpsimd.indirect_dma_start(out=slots_d, out_offset=bass.IndirectOffsetOnAxis(ap=slot_i[:, b, k:k + 1], axis=0),
                                                 in_=stage[b % 4], in_offset=None).then_inc(scattered[b % 4], 16)
            pool.wait_ge(y_stored[0], 16 * ((TILES + 1) // 2))
            pool.wait_ge(y_stored[1], 16 * (TILES // 2))
            for b in range(B):
                for k in range(TOP):
                    nc.gpsimd.indirect_dma_start(out=yg[b][k], out_offset=None, in_=y_d,
                                                 in_offset=bass.IndirectOffsetOnAxis(ap=slot_i[:, b, k:k + 1], axis=0)).then_inc(gathered[b], 16)
    return nc


def _consts():
    import numpy as np

    c = np.zeros((P, CONST_W), np.float32)
    p = np.arange(P)[:, None]

    def put(name, v):
        at, width = CONST[name]
        c[:, at:at + width] = v

    put("ident", p == np.arange(P))
    put("headmask", p // D == np.arange(HG))
    put("parmask", (p // D) % 2 == np.arange(2))
    put("lower", p < np.arange(TQ))
    put("expert", np.arange(NE) - NE)
    put("below", (np.arange(NE) <= np.arange(NE)[:, None]).reshape(1, -1))
    put("tile", np.arange(TILES))
    put("sel", (p % 32 == np.arange(NE)) & (p < 96))
    return c


def _layout(inp):
    import numpy as np

    f = {k: np.asarray(v) for k, v in inp.items()}
    rows = lambda a: np.ascontiguousarray(a.reshape(-1, P, a.shape[-1]).transpose(1, 0, 2))
    col = lambda a: np.ascontiguousarray(a.reshape(-1, P).T)

    def experts(w1, w2):
        a = w1.transpose(0, 2, 1).reshape(-1, EC, P, FF).transpose(0, 2, 1, 3).reshape(-1, P, EC * FF)
        b = w2.transpose(0, 2, 1).reshape(-1, FC, P, E).transpose(0, 2, 1, 3).reshape(-1, P, FC * E)
        ab = np.concatenate([a, b], axis=2).reshape(-1, P, 4, WE // 4).transpose(0, 2, 1, 3)
        return np.ascontiguousarray(ab.reshape(-1, P, WE // 4))

    ctxT = f["ctx_1024"].transpose(0, 2, 1).reshape(B, EC, P, TK).transpose(0, 2, 1, 3)
    return {
        "x": f["x"], "ctxT": np.ascontiguousarray(ctxT),
        "wq": rows(f["L0_xattn_Wq"]), "wkv": rows(f["L0_xattn_Wkv"]), "wo": rows(f["L0_xattn_Wo"]),
        "bq": col(f["L0_xattn_bq"]), "bk": col(f["L0_xattn_bkv"][:E]), "bv": f["L0_xattn_bkv"][E:], "bo": f["L0_xattn_bo"],
        "gates": np.concatenate([f["g_xattn"], f["g_ffn"]]),
        "w": experts(f["L0_ffn_spec_w1"], f["L0_ffn_spec_w2"]), "b1": f["L0_ffn_spec_b1"], "b2": f["L0_ffn_spec_b2"],
        "ws": experts(f["L0_ffn_shared_w1"][None], f["L0_ffn_shared_w2"][None]), "b1s": col(f["L0_ffn_shared_b1"]), "b2s": f["L0_ffn_shared_b2"],
        "rw": rows(np.ascontiguousarray(f["L0_ffn_router_w"].T)), "rb": f["L0_ffn_router_b"],
        "consts": _consts(),
    }


def kernel(**inputs):
    import numpy as np
    import concourse.bacc as bacc
    from concourse.bass_utils import run_bass_kernel_spmd as run

    nc = bacc.Bacc("TRN2", target_bir_lowering=False, num_devices=1)
    arrays, args = {}, []
    for name, a in _layout(inputs).items():
        a = np.ascontiguousarray(a)
        arrays[f"in_{name}"] = a
        args.append(nc.dram_tensor(f"in_{name}", a.shape, mybir.dt.from_np(a.dtype), kind="ExternalInput").ap())
    args.append(nc.dram_tensor("out_0", (B, TQ, E), F32, kind="ExternalOutput").ap())
    build(nc, *args)
    r = run(nc, [arrays], core_ids=[0])
    return r.results[0]["out_0"]
```

```python
from contextlib import ExitStack

import concourse.bass as bass
from concourse import mybir

F32 = mybir.dt.float32
BF16 = mybir.dt.bfloat16
I32 = mybir.dt.int32
ALU = mybir.AluOpType
ACT = mybir.ActivationFunctionType
AX = mybir.AxisListType

P = 128
B, TQ, E = 16, 112, 256
TK, H, D = 375, 16, 16
EC = E // P
G, HG = 2, 8
KT, KR = 3, 125
UNITS = G * KT
NE, FF = 8, 1024
FC = FF // P
SHARED = NE
WE = EC * FF + FC * E
TOP = 2
TILES = (B * TQ * TOP) // P + NE - 1
SLOTS = TILES * P
CH = 2 * TQ
EPS = 1e-5
RING = 4


def columns(*parts):
    at, out = 0, {}
    for name, width in parts:
        out[name] = (at, width)
        at += width
    return out, at


CONST, CONST_W = columns(("ident", P), ("headmask", HG), ("parmask", 2))
ROUTE, ROUTE_W = columns(("lower", TQ), ("expert", NE), ("below", NE * NE), ("tile", TILES))


def build(nc, x, ctxT, wq, wkv, wo, bq, bk, bv, bo, gates, w, b1, b2, ws, b1s, b2s, rw, rb, consts, route, out):
    slots_d = nc.dram_tensor("slots_d", [SLOTS, E], F32).ap()
    y_d = nc.dram_tensor("y_d", [SLOTS, E], F32).ap()
    xn2_d = nc.dram_tensor("xn2_d", [B, TQ, E], F32).ap()

    with ExitStack() as ctx:
        def sb(name, shape, dt=F32):
            return ctx.enter_context(nc.sbuf_tensor(name, shape, dt))

        def sem(name):
            return ctx.enter_context(nc.semaphore(name))

        W = sb("W", [P, NE + 1, WE])
        xall = sb("xall", [TQ, B, E])
        xn2T = sb("xn2T", [P, EC, B * TQ])
        cst = sb("cst", [P, CONST_W])
        b1_s = sb("b1_s", [P, NE * FC])
        b2_s = sb("b2_s", [P, NE, E])
        small = sb("small", [P, 64])
        work = sb("work", [P, 6144])

        def const(name):
            at, width = CONST[name]
            return cst[:, at:at + width]

        def route_const(name):
            at, width = ROUTE[name]
            return rcst[:, at:at + width]

        ident = const("ident")

        class Region:

            def __init__(self, whole):
                self.whole, self.at = whole, 0

            def take(self, rows, *dims):
                n = 1
                for d in dims:
                    n *= d
                v = self.whole[0:rows, self.at:self.at + n]
                self.at += n
                assert self.at <= self.whole.shape[1]
                if len(dims) == 2:
                    return v.rearrange("p (a b) -> p a b", a=dims[0])
                if len(dims) == 3:
                    return v.rearrange("p (a b c) -> p a b c", a=dims[0], b=dims[1])
                return v

        late = Region(W[:, NE // 2:NE, :].rearrange("p e n -> p (e n)"))
        wq_s = late.take(P, EC, E)
        wkv_s = late.take(P, EC, 2 * E)
        wo_s = late.take(P, EC, E)
        ctx_at = late.at
        ctx_s = [late.take(P, EC, TK) for _ in range(2)]
        kT = [late.take(P, G, TK) for _ in range(2)]
        V = [late.take(KR, KT, E) for _ in range(2)]
        qbd = [late.take(P, G, HG, TQ) for _ in range(2)]
        prob = [late.take(KR, HG, TQ) for _ in range(RING)]
        qs = [late.take(P, G, TQ) for _ in range(2)]
        otmp = late.take(P, G, TQ)
        oT = late.take(P, G, TQ)
        zeros = late.take(P, E)
        early = Region(work[:, 0:FC * CH * 2])
        xn = [early.take(TQ, E) for _ in range(2)]
        xn2 = [early.take(TQ, E) for _ in range(2)]
        x2 = [early.take(TQ, E) for _ in range(2)]
        xnT = early.take(P, EC, TQ)
        vs = [early.take(KR, P) for _ in range(RING)]
        bvb = early.take(KR, E)
        bob = early.take(TQ, E)
        b2b = early.take(TQ, E)
        mx = [early.take(KR, HG) for _ in range(2)]
        zz = [early.take(KR, HG) for _ in range(2)]
        rz = [early.take(KR, HG) for _ in range(2)]
        st1, mv1 = early.take(TQ, B, 6), early.take(TQ, B, 2)
        ve1, rstd1 = early.take(TQ, B), early.take(TQ, B)
        st2, mv2 = early.take(TQ, 6), early.take(TQ, 2)
        ve2, rstd2 = early.take(TQ, 1), early.take(TQ, 1)

        hT = [work[:, k * FC * CH:(k + 1) * FC * CH] for k in range(2)]
        hTs = [v.rearrange("p (f t) -> p f t", f=FC) for v in hT]
        hTe = [v[:, 0:FF].rearrange("p (f t) -> p f t", f=FC) for v in hT]
        ys = [v[:, FF:FF + E] for v in hT]
        xT = [v[:, FF + E:FF + 2 * E].rearrange("p (c t) -> p c t", c=EC) for v in hT]
        tail = Region(work[:, 2 * FC * CH:])
        xg = [tail.take(P, E) for _ in range(2)]
        h = [tail.take(P, FF) for _ in range(2)]
        stage = [xg[0][0:TQ], xg[1][0:TQ], h[1][0:TQ, 512:768], h[1][0:TQ, 768:1024]]
        scratch = Region(work[:, 2 * FC * CH + 2 * E:2 * FC * CH + 2 * E + FF + 512])
        bne = lambda: scratch.take(TQ, B, NE)
        lg, pr, oh1, oh2, t1, t2 = bne(), bne(), bne(), bne(), bne(), bne()
        teq = scratch.whole[0:1, 0:TILES * (NE - 1)].rearrange("t (i e) -> t i e", e=NE - 1)
        assert TILES * (NE - 1) <= 2 * B * NE
        hits = scratch.take(TQ, B * NE // 2).bitcast(BF16)
        lower_b = scratch.take(TQ, TQ // 2).bitcast(BF16)
        ones_b = scratch.take(TQ, TQ // 2).bitcast(BF16)
        bv_ = lambda: scratch.take(TQ, B)
        lmax, lsum, p1, p2, i1, i2 = bv_(), bv_(), bv_(), bv_(), bv_(), bv_()
        cnt, end, base = scratch.take(TQ, NE), scratch.take(TQ, NE), scratch.take(TQ, NE)
        cnt_i = scratch.take(TQ, NE).bitcast(I32)
        prod = scratch.take(TQ, NE, NE)
        tef = scratch.take(1, TILES)
        slot_f = scratch.take(TQ, B, TOP)
        rcst = scratch.take(TQ, ROUTE_W)
        cw = sb("cw", [TQ, TOP, B])
        slot_i = sb("slot_i", [TQ, B, TOP], I32)
        tile_e = sb("tile_e", [1, TILES], I32)
        done = Region(W[:, 0:2, :].rearrange("p e n -> p (e n)"))
        yg = [[done.take(TQ, E) for _ in range(TOP)] for _ in range(B)]

        bq_s, bk_s, b1s_s, bq4 = small[:, 0:2], small[:, 2:4], small[:, 4:12], small[:, 12:14]
        gate_in, tg = small[0:TQ, 14:16], small[0:TQ, 16:18]
        mhalf = small[0:TQ, 18:19]
        rbb = small[0:TQ, 20:28]
        rw_s = small[:, 28:44].rearrange("p (c e) -> p c e", c=EC)

        bank = ctx.enter_context(nc.psum_tensor("bank", [P, 8, 512], F32))
        S = [bank[0:KR, 2 * k:2 * k + 2, 0:4 * TQ] for k in range(2)]
        O = bank[:, 4, :]
        J = [bank[:, 5 + k, :] for k in range(3)]
        Hp = [bank[:, 2 * k:2 * k + 2, :] for k in range(2)]
        HTp = bank[:, 4:6, :]
        XTp, Yp = bank[:, 6, :], bank[:, 7, :]

        in_ctx, in_xn = late.whole[:, ctx_at:ctx_at + 2 * EC * TK], work[:, 0:2 * E]
        LOGITS = [(4 * k, 4, in_ctx[0:NE, 4 * k * TQ:4 * (k + 1) * TQ], J[1 - k % 2]) for k in range(3)]
        LOGITS += [(B - 4, 3, in_xn[0:NE, 0:3 * TQ], bank[:, 0, :]), (B - 1, 1, in_xn[0:NE, 3 * TQ:4 * TQ], bank[:, 1, :])]

        cst_in, gates_in, small_in = sem("cst_in"), sem("gates_in"), sem("small_in")
        wkv_in, wq_in, wo_in = sem("wkv_in"), sem("wq_in"), sem("wo_in")
        x_in = [sem(f"x_in{k}") for k in range(4)]
        ctx_in = [sem("ctx_in0"), sem("ctx_in1")]
        w_in, ws_in = sem("w_in"), sem("ws_in")
        xn2_stored = [sem("xn2_stored0"), sem("xn2_stored1")]
        setup_dve, setup_act = sem("setup_dve"), sem("setup_act")
        zeroed, bias_in, route_in = sem("zeroed"), sem("bias_in"), sem("route_in")
        slots_zeroed, router_in = sem("slots_zeroed"), sem("router_in")
        var1, rstd1_ready, xn_ready = sem("var1"), sem("rstd1_ready"), sem("xn_ready")
        xnT_ps, xnT_sb, q_ps, qs_sb, qbd_ready = sem("xnT_ps"), sem("xnT_sb"), sem("q_ps"), sem("qs_sb"), sem("qbd_ready")
        k_ps, k_sb, v_ps, v_sb = sem("k_ps"), sem("k_sb"), sem("v_ps"), sem("v_sb")
        qk_done, max_done, sub_done, exp_done = sem("qk_done"), sem("max_done"), sem("sub_done"), sem("exp_done")
        sum_done, rz_ready, vs_ready, pv_done = sem("sum_done"), sem("rz_ready"), sem("vs_ready"), sem("pv_done")
        otmp_ready, oT_ready, op_ps, x2_ready = sem("otmp_ready"), sem("oT_ready"), sem("op_ps"), sem("x2_ready")
        xbo_ready, b2_added = sem("xbo_ready"), sem("b2_added")
        st2_ready, mv2_ready, ve2_ready, rstd2_ready = sem("st2_ready"), sem("mv2_ready"), sem("ve2_ready"), sem("rstd2_ready")
        xn2_ready, xn2T_ps, xn2T_sb = sem("xn2_ready"), sem("xn2T_ps"), sem("xn2T_sb")
        lgT_ps, lgT_sb, lg_ps = sem("lgT_ps"), sem("lgT_sb"), sem("lg_ps")
        rt, rt_exp_in, rt_exp, hits_ready, ranks_ps, routed = (sem("rt"), sem("rt_exp_in"), sem("rt_exp"), sem("hits_ready"),
                                                              sem("ranks_ps"), sem("routed"))
        staged, scattered = [sem(f"staged{k}") for k in range(4)], [sem(f"scattered{k}") for k in range(4)]
        l1s_ps, hTs_sb, l2s_ps, shared_done = sem("l1s_ps"), sem("hTs_sb"), sem("l2s_ps"), sem("shared_done")
        xg_in = [sem("xg_in0"), sem("xg_in1")]
        xT_ps, xT_sb, l1_ps, h_sb, t_ps, hT_sb, l2_ps, y_sb = (sem("xT_ps"), sem("xT_sb"), sem("l1_ps"), sem("h_sb"),
                                                              sem("t_ps"), sem("hT_sb"), sem("l2_ps"), sem("y_sb"))
        y_stored = [sem("y_stored0"), sem("y_stored1")]
        gathered = [sem(f"gathered{b}") for b in range(B)]
        comb1, comb2, out_stored = sem("comb1"), sem("comb2"), sem("out_stored")

        class Step:

            def __init__(self, half, par):
                self.half, self.par, self.b = half, par, half * 2 + par

            def has(self, lo, hi):
                return not isinstance(self.b, int) or lo <= self.b <= hi

            def halves(self, off):
                return self.half + (self.par + off) // 2

        def ring(par, u):
            return (UNITS * par + u) % RING

        def phase1(engine, step):
            for b in range(-1, 4):
                step(Step(b // 2, b % 2))
            with engine.Fori(2, B // 2 - 1) as half:
                for par in range(2):
                    step(Step(half, par))
            for b in range(B - 2, B + 2):
                step(Step(b // 2, b % 2))

        def tiles_loop(engine, tile_step):
            for k in range(2):
                tile_step(0, k)
            with engine.Fori(1, (TILES - 3) // 2) as half:
                for k in range(2):
                    tile_step(half, k)

        def wait(engine, s, value):
            if not isinstance(value, int) or value > 0:
                engine.wait_ge(s, value)

        block = ctx.enter_context(nc.Block())

        @block.sync
        def _(sp):
            def load_x(k):
                sp.dma_start(xall[:, 4 * k:4 * k + 4, :], x[4 * k:4 * k + 4].rearrange("b t e -> t b e")).then_inc(x_in[k], 16)

            load_x(0)
            sp.dma_start(ctx_s[0], ctxT[0]).then_inc(ctx_in[0], 16)
            sp.dma_start(wkv_s, wkv).then_inc(wkv_in, 16)
            sp.dma_start(cst[:, :], consts).then_inc(cst_in, 16)
            sp.dma_start(wq_s, wq).then_inc(wq_in, 16)
            load_x(1)
            sp.dma_start(ctx_s[1], ctxT[1]).then_inc(ctx_in[1], 16)
            load_x(2)
            load_x(3)
            sp.dma_start(wo_s, wo).then_inc(wo_in, 16)
            for dst, src in ((b1s_s, b1s), (rw_s, rw), (rbb, rb.partition_broadcast(TQ))):
                sp.dma_start(dst, src).then_inc(router_in, 16)
            pieces = W[:, :, :].rearrange("p e (q n) -> p (e q) n", q=4)

            def load_for_later(b):
                sp.dma_start(W[:, SHARED, b * 1024:(b + 1) * 1024], ws[b]).then_inc(ws_in, 16)
                if b == 1:
                    sp.dma_start(rcst, route[0:TQ]).then_inc(route_in, 16)
                    sp.dma_start(b1_s[:, :], b1).then_inc(bias_in, 16)
                if b == 2:
                    sp.dma_start(b2_s[:, :, :].rearrange("p e n -> p (e n)"), b2.partition_broadcast(P)).then_inc(bias_in, 16)
                if b == 3:
                    sp.wait_ge(zeroed, 1)
                    sp.dma_start(slots_d.rearrange("(t p) e -> p t e", p=P),
                                 zeros.unsqueeze(1).to_broadcast([P, TILES, E])).then_inc(slots_zeroed, 16)

            def step(s):
                b = s.b
                if s.has(0, B - 3):
                    sp.wait_ge(v_ps, 2 * b + 2)
                    sp.dma_start(ctx_s[s.par], ctxT[bass.ds(b + 2, 1)].rearrange("a p c k -> (a p) c k")
                                 ).then_inc(ctx_in[s.par], 16)
                if s.has(-1, B - 2):
                    sp.dma_start(pieces[:, bass.ds(b + 1, 1), :], w[bass.ds(b + 1, 1)].rearrange("a p n -> p a n")
                                 ).then_inc(w_in, 16)
                if isinstance(b, int) and 0 <= b < 4:
                    load_for_later(b)
                if s.has(2, B + 1):
                    sp.wait_ge(xn2_ready, b - 1)
                    sp.dma_start(xn2_d[bass.ds(b - 2, 1)].rearrange("a t e -> (a t) e"), xn2[s.par]
                                 ).then_inc(xn2_stored[s.par], 16)

            phase1(sp, step)

            def stage_rows(b):
                if b >= 4:
                    sp.wait_ge(scattered[b % 4], 32 * (b // 4))
                sp.dma_start(stage[b % 4], xn2_d[b]).then_inc(staged[b % 4], 16)

            for k in range(2):
                sp.wait_ge(xn2_stored[k], 16 * (B // 2 - 1))
            for b in range(4):
                stage_rows(b)
            sp.wait_ge(op_ps, B)
            sp.wait_ge(lg_ps, 3)
            sp.wait_ge(slots_zeroed, 16)
            for k in range(16, 26):
                sp.dma_start(pieces[:, k, :], w[k]).then_inc(w_in, 16)
            for k in range(2):
                sp.wait_ge(xn2_stored[k], 16 * B // 2)
            for b in range(4, B):
                stage_rows(b)
                if 22 + b < 32:
                    sp.dma_start(pieces[:, 22 + b, :], w[22 + b]).then_inc(w_in, 16)

            for k in range(4):
                sp.wait_ge(scattered[k], 32 * (B // 4))

            def load_rows(i, par):
                sp.dma_start(xg[par], slots_d[bass.ds(i * P, P), :]).then_inc(xg_in[par], 16)

            def store_rows(i, par):
                sp.wait_ge(y_sb, i + 1)
                sp.dma_start(y_d[bass.ds(i * P, P), :], ys[par]).then_inc(y_stored[par], 16)

            load_rows(0, 0)
            load_rows(1, 1)
            for i in range(2, 5):
                sp.wait_ge(xT_ps, i - 1)
                load_rows(i, i % 2)
            with sp.Fori(1, (TILES - 3) // 2) as half:
                for par in range(2):
                    i = half * 2 + par
                    sp.wait_ge(xT_ps, i + 2)
                    load_rows(i + 3, 1 - par)
                    store_rows(i - 2, par)
            for i in range(TILES - 5, TILES):
                store_rows(i, i % 2)
            for b in range(0, B, 2):
                sp.wait_ge(comb2, b + 2)
                sp.wait_ge(shared_done, b + 2)
                sp.dma_start(out[b:b + 2].rearrange("b t e -> t b e"), xall[:, b:b + 2, :]).then_inc(out_stored, 16)
            sp.wait_ge(out_stored, 16 * B // 2)

        @block.tensor
        def _(pe):
            mm = nc.tensor.matmul

            def scores(s, u):
                g, kt, n = u // KT, u % KT, 6 * s.b + u
                if kt == 0:
                    pe.wait_ge(qbd_ready, 2 * s.b + g + 1)
                    pe.wait_ge(k_sb, 2 * s.b + g + 1)
                if u % 2 == 0:
                    wait(pe, exp_done, n - 1)
                else:
                    wait(pe, sub_done, 3 * s.b + (u - 1) // 2)
                for a in range(2):
                    last = mm(S[u % 2][:, a, :], kT[s.par][:, g, kt * KR:(kt + 1) * KR],
                              qbd[s.par][:, g, 4 * a:4 * a + 4, :], start=True, stop=True)
                last.then_inc(qk_done, 1)

            def values(b, par, u):
                g, kt, n = u // KT, u % KT, 6 * b + u
                pe.wait_ge(exp_done, n + 1)
                pe.wait_ge(vs_ready, n + 1)
                if u == 0:
                    wait(pe, oT_ready, b)
                for j in range(4):
                    last = mm(O[32 * j:32 * j + 32, g * 2 * TQ:(g + 1) * 2 * TQ], vs[ring(par, u)][:, 32 * j:32 * j + 32],
                              prob[ring(par, u)][:, 2 * j:2 * j + 2, :], start=(kt == 0), stop=(kt == KT - 1),
                              tile_position=(0, 32 * j), skip_group_check=True)
                last.then_inc(pv_done, 1)

            def logits(k):
                first, n, _, at = LOGITS[k]
                if k == 2:
                    pe.wait_ge(lgT_sb, 1)
                for c in range(EC):
                    last = mm(at[0:NE, 0:n * TQ], rw_s[:, c, :], xn2T[:, c, first * TQ:(first + n) * TQ],
                              start=(c == 0), stop=(c == EC - 1))
                last.then_inc(lgT_ps, 1)

            def turn_logits(k):
                first, n, rows, _ = LOGITS[k]
                pe.wait_ge(lgT_sb, max(k, 2) + 1)
                for b in range(n):
                    last = nc.tensor.transpose(J[1][0:TQ, (first + b) * NE:(first + b + 1) * NE], rows[:, b * TQ:(b + 1) * TQ], ident[0:NE, 0:NE])
                last.then_inc(lg_ps, 1)

            def turn_x(s):
                b, nxt, npar = s.b, s.b + 1, 1 - s.par
                pe.wait_ge(xn_ready, nxt + 1)
                if isinstance(b, int) and b < 0:
                    pe.wait_ge(cst_in, 16)
                wait(pe, v_sb, 2 * b + 2)
                for c in range(EC):
                    last = nc.tensor.transpose(J[1][:, c * TQ:(c + 1) * TQ], xn[npar][:, c * P:(c + 1) * P], ident[0:TQ, 0:TQ])
                last.then_inc(xnT_ps, 1)

            def project_k(s, groups=range(G)):
                b, nxt, npar = s.b, s.b + 1, 1 - s.par
                pe.wait_ge(ctx_in[npar], (s.halves(1) + 1) * 16)
                if isinstance(b, int) and b < 0:
                    pe.wait_ge(wkv_in, 16)
                for g in groups:
                    if g == 0:
                        wait(pe, v_sb, 2 * b + 1)
                    else:
                        wait(pe, xn2T_sb, b - 2)
                    for c in range(EC):
                        last = mm(J[2 * g][:, 0:TK], wkv_s[:, c, g * P:(g + 1) * P], ctx_s[npar][:, c, :],
                                  start=(c == 0), stop=(c == EC - 1))
                    last.then_inc(k_ps, 1)

            def step(s):
                b, nxt, npar = s.b, s.b + 1, 1 - s.par
                attend, prep = s.has(0, B - 1), s.has(-1, B - 2)
                prev, prev2 = s.has(1, B), s.has(2, B + 1)
                first = isinstance(b, int) and b < 0
                if attend:
                    scores(s, 0)
                if first:
                    project_k(s, (0,))
                if prep:
                    turn_x(s)
                if first:
                    project_k(s, (1,))
                if prev:
                    values(b - 1, npar, 3)
                if attend:
                    scores(s, 1)
                if prep and not first:
                    project_k(s)
                if isinstance(b, int) and b == B - 1:
                    pe.wait_ge(v_sb, 2 * B)
                    pe.wait_ge(xn2T_sb, 12)
                    pe.wait_ge(router_in, 48)
                    logits(0)
                if isinstance(b, int) and b == B:
                    logits(2)
                if prev:
                    values(b - 1, npar, 4)
                if prev:
                    values(b - 1, npar, 5)
                if attend:
                    scores(s, 2)
                if prep:
                    if isinstance(b, int) and b < 0:
                        pe.wait_ge(wq_in, 16)
                    pe.wait_ge(xnT_sb, nxt + 1)
                    for g in range(G):
                        for c in range(EC):
                            last = mm(J[1][:, g * TQ:(g + 1) * TQ], wq_s[:, c, g * P:(g + 1) * P], xnT[:, c, :],
                                      start=(c == 0), stop=(c == EC - 1))
                    last.then_inc(q_ps, 1)
                if prep:
                    pe.wait_ge(k_sb, 2 * b + 3)
                    for kt in range(2):
                        for c in range(EC):
                            last = mm(J[0][0:KR, kt * E:(kt + 1) * E], ctx_s[npar][:, c, kt * KR:(kt + 1) * KR],
                                      wkv_s[:, c, E:2 * E], start=(c == 0), stop=(c == EC - 1))
                    last.then_inc(v_ps, 1)
                if attend:
                    values(b, s.par, 0)
                    scores(s, 3)
                if isinstance(b, int) and b == B - 1:
                    logits(1)
                if attend:
                    values(b, s.par, 1)
                    scores(s, 4)
                if prev:
                    pe.wait_ge(oT_ready, b)
                    if prep:
                        pe.wait_ge(k_sb, 2 * b + 4)
                    else:
                        wait(pe, xn2T_sb, b - 2)
                    if isinstance(b, int) and b == 1:
                        pe.wait_ge(wo_in, 16)
                    for g in range(G):
                        last = mm(J[2][0:TQ, 0:E], oT[:, g, :], wo_s[:, g, :], start=(g == 0), stop=(g == G - 1))
                    last.then_inc(op_ps, 1)
                if isinstance(b, int) and b == B:
                    for k in range(3):
                        turn_logits(k)
                if isinstance(b, int) and b == B + 1:
                    pe.wait_ge(xn2T_sb, B - 1)
                    logits(3)
                if prep:
                    pe.wait_ge(qs_sb, b + 2)
                    for c in range(EC):
                        last = mm(J[1][0:KR, 0:E], ctx_s[npar][:, c, 2 * KR:3 * KR], wkv_s[:, c, E:2 * E],
                                  start=(c == 0), stop=(c == EC - 1))
                    last.then_inc(v_ps, 1)
                if attend:
                    values(b, s.par, 2)
                    scores(s, 5)
                if prev2:
                    pe.wait_ge(xn2_ready, b - 1)
                    if prev:
                        pe.wait_ge(x2_ready, b)
                    else:
                        pe.wait_ge(xn2T_sb, b - 2)
                    for c in range(EC):
                        last = nc.tensor.transpose(J[2][:, c * TQ:(c + 1) * TQ], xn2[s.par][:, c * P:(c + 1) * P], ident[0:TQ, 0:TQ])
                    last.then_inc(xn2T_ps, 1)

            phase1(pe, step)

            pe.wait_ge(xn2T_sb, B)
            logits(4)
            turn_logits(3)
            turn_logits(4)

            def shared_hidden(n):
                for f in range(FC):
                    if f % 2 == 0:
                        wait(pe, hTs_sb, FC * n - FC + f + 2)
                    for c in range(EC):
                        last = mm(bank[:, f // 2, (f % 2) * CH:(f % 2 + 1) * CH],
                                  W[:, SHARED, c * FF + f * P:c * FF + (f + 1) * P],
                                  xn2T[:, c, bass.ds(n * CH, CH)], start=(c == 0), stop=(c == EC - 1))
                    if f % 2 == 1:
                        last.then_inc(l1s_ps, 1)

            def shared_out(n, par):
                pe.wait_ge(hTs_sb, FC * n + FC)
                for k in range(2):
                    wait(pe, shared_done, 2 * n - 1 + k)
                    for f in range(FC):
                        last = mm(HTp[0:TQ, k, 0:E], hTs[par][:, f, k * TQ:(k + 1) * TQ],
                                  W[:, SHARED, EC * FF + f * E:EC * FF + (f + 1) * E], start=(f == 0), stop=(f == FC - 1))
                    last.then_inc(l2s_ps, 1)

            pe.wait_ge(ws_in, 64)
            def ranks():
                pe.wait_ge(hits_ready, 1)
                R = XTp[0:TQ, 0:(B + 1) * NE]
                mm(R[:, 0:B * NE], lower_b, hits, start=True, stop=False, skip_group_check=True)
                for b in range(B):
                    last = mm(R[:, (b + 1) * NE:].rearrange("t (b e) -> t b e", e=NE), ones_b,
                              hits[:, b * NE:(b + 1) * NE].unsqueeze(1).to_broadcast([TQ, B - b, NE]),
                              start=False, stop=(b == B - 1), skip_group_check=True)
                last.then_inc(ranks_ps, 1)
            shared_hidden(0)
            ranks()
            shared_hidden(1)
            for par in range(2):
                shared_out(par, par)
            for par in range(2):
                shared_hidden(2 + par)
            for par in range(2):
                shared_out(2 + par, par)

            def turn_rows(i, par):
                wait(pe, xT_sb, i)
                for c in range(EC):
                    last = nc.tensor.transpose(XTp[:, c * P:(c + 1) * P], xg[par][:, c * P:(c + 1) * P], ident)
                last.then_inc(xT_ps, 1)

            def hidden(i, par):
                e = nc.tensor.value_load(tile_e[0:1, bass.ds(i, 1)], min_val=0, max_val=NE - 1)
                pe.wait_ge(xT_sb, i + 1)
                wait(pe, h_sb, i - 1)
                for a in range(2):
                    for c in range(EC):
                        last = mm(Hp[par][:, a, :], xT[par][:, c, :],
                                  W[:, bass.ds(e, 1), c * FF + a * 512:c * FF + (a + 1) * 512].rearrange("p a n -> p (a n)"),
                                  start=(c == 0), stop=(c == EC - 1))
                last.then_inc(l1_ps, 1)

            def turn_hidden(i, par):
                pe.wait_ge(h_sb, i + 1)
                for a in range(2):
                    wait(pe, hT_sb, 2 * i - 1 + a)
                    for f in range(4):
                        last = nc.tensor.transpose(HTp[:, a, f * P:(f + 1) * P], h[par][:, (4 * a + f) * P:(4 * a + f + 1) * P], ident)
                    last.then_inc(t_ps, 1)

            def result(i, par):
                e = nc.tensor.value_load(tile_e[0:1, bass.ds(i, 1)], min_val=0, max_val=NE - 1)
                wait(pe, y_sb, i)
                pe.wait_ge(hT_sb, 2 * i + 1)
                for f in range(FC):
                    if f == 4:
                        pe.wait_ge(hT_sb, 2 * i + 2)
                    last = mm(Yp[:, 0:E], hTe[par][:, f, :],
                              W[:, bass.ds(e, 1), EC * FF + f * E:EC * FF + (f + 1) * E].rearrange("p a n -> p (a n)"),
                              start=(f == 0), stop=(f == FC - 1))
                last.then_inc(l2_ps, 1)

            pe.wait_ge(w_in, 16 * 32)
            pe.wait_ge(xg_in[0], 16)
            pe.wait_ge(hTs_sb, 4 * FC)
            pe.wait_ge(shared_done, 8)
            turn_rows(0, 0)
            pe.wait_ge(xg_in[1], 16)
            turn_rows(1, 1)
            hidden(0, 0)
            pe.wait_ge(xg_in[0], 32)
            turn_rows(2, 0)
            hidden(1, 1)
            turn_hidden(0, 0)

            def tile_step(half, k):
                i, par = half * 2 + 1 + k, (1 + k) % 2
                pe.wait_ge(xg_in[par], (half + (k + 3) // 2 + 1) * 16)
                turn_rows(i + 2, par)
                hidden(i + 1, 1 - par)
                turn_hidden(i, par)
                result(i - 1, 1 - par)

            tiles_loop(pe, tile_step)
            i = TILES - 2
            hidden(i + 1, (i + 1) % 2)
            turn_hidden(i, i % 2)
            result(i - 1, (i - 1) % 2)
            turn_hidden(i + 1, (i + 1) % 2)
            result(i, i % 2)
            result(i + 1, (i + 1) % 2)
            with pe.Fori(2, 4) as pair:
                for par in range(2):
                    shared_hidden(pair * 2 + par)
                for par in range(2):
                    shared_out(pair * 2 + par, par)

        @block.scalar
        def _(act):
            for dst, src in ((gate_in, gates.partition_broadcast(TQ)), (bq_s, bq), (bk_s, bk)):
                act.dma_start(dst, src).then_inc(gates_in, 16)
            for dst, src in ((bob, bo.partition_broadcast(TQ)), (b2b, b2s.partition_broadcast(TQ)), (bvb, bv.partition_broadcast(KR))):
                act.dma_start(dst, src).then_inc(small_in, 16)
            act.wait_ge(gates_in, 16 * 3)
            nc.scalar.activation(tg, gate_in, ACT.Tanh).then_inc(setup_act, 1)
            nc.scalar.activation(bq4, bq_s, ACT.Copy, scale=1.0 / D ** 0.5).then_inc(setup_act, 1)
            act.wait_ge(setup_act, 2)

            def copy_logits(k):
                act.wait_ge(lgT_ps, k + 1)
                nc.scalar.activation(LOGITS[k][2], LOGITS[k][3][0:NE, 0:LOGITS[k][1] * TQ], ACT.Copy).then_inc(lgT_sb, 1)

            def exps(s, u):
                n = 6 * s.b + u
                if u % 2 == 0:
                    wait(act, pv_done, n + 1 - RING)
                    act.wait_ge(max_done, n + 1)
                    for hh in range(HG):
                        last = nc.scalar.activation(prob[ring(s.par, u)][:, hh, :], S[0][:, hh // 4, (hh % 4) * TQ:(hh % 4 + 1) * TQ],
                                                    ACT.Exp, bias=mx[0][:, hh:hh + 1], accum_out=zz[0][:, hh:hh + 1])
                    last.then_inc(exp_done, 1)
                else:
                    act.wait_ge(sub_done, 3 * s.b + (u + 1) // 2)
                    nc.scalar.activation(prob[ring(s.par, u)], prob[ring(s.par, u)], ACT.Exp).then_inc(exp_done, 1)

            def step(s):
                b, nxt, npar = s.b, s.b + 1, 1 - s.par
                attend, prep, prev2 = s.has(0, B - 1), s.has(-1, B - 2), s.has(2, B + 1)
                for u in range(UNITS):
                    if u == 2 and prep:
                        act.wait_ge(q_ps, nxt + 1)
                        wait(act, qbd_ready, 2 * b)
                        for g in range(G):
                            last = nc.scalar.activation(qs[npar][:, g, :], J[1][:, g * TQ:(g + 1) * TQ], ACT.Identity,
                                                        bias=bq4[:, g:g + 1], scale=1.0 / D ** 0.5)
                        last.then_inc(qs_sb, 1)
                    if attend:
                        exps(s, u)
                    if u in (2, 4) and isinstance(b, int) and b == B - 1:
                        copy_logits(u // 2 - 1)
                    if u == 0 and prep:
                        act.wait_ge(xnT_ps, nxt + 1)
                        wait(act, q_ps, nxt)
                        nc.scalar.activation(xnT, J[1][:, 0:EC * TQ].rearrange("p (c t) -> p c t", c=EC), ACT.Copy
                                             ).then_inc(xnT_sb, 1)
                    if u == 1 and prep:
                        for g in range(G):
                            act.wait_ge(k_ps, 2 * nxt + g + 1)
                            nc.scalar.activation(kT[npar][:, g, :], J[2 * g][:, 0:TK], ACT.Identity, bias=bk_s[:, g:g + 1]
                                                 ).then_inc(k_sb, 1)
                if isinstance(b, int) and b == B:
                    copy_logits(2)
                if isinstance(b, int) and b == B + 1:
                    copy_logits(3)
                if prev2:
                    act.wait_ge(xn2T_ps, b - 1)
                    nc.scalar.activation(xn2T[:, :, bass.ds((b - 2) * TQ, TQ)],
                                         J[2][:, 0:EC * TQ].rearrange("p (c t) -> p c t", c=EC), ACT.Copy).then_inc(xn2T_sb, 1)

            phase1(act, step)
            copy_logits(4)
            act.wait_ge(rt_exp_in, 1)
            nc.scalar.activation(pr, lg, ACT.Exp).then_inc(rt_exp, 1)
            act.wait_ge(b2_added, B)
            for k in range(2):
                act.wait_ge(xn2_stored[k], 16 * B // 2)

            def shared_gelu(n, par):
                wait(act, l2s_ps, 2 * n - 2)
                for f in range(FC):
                    act.wait_ge(l1s_ps, 4 * n + f // 2 + 1)
                    nc.scalar.activation(hTs[par][:, f, :], bank[:, f // 2, (f % 2) * CH:(f % 2 + 1) * CH],
                                         ACT.Gelu_apprx_tanh, bias=b1s_s[:, f:f + 1]).then_inc(hTs_sb, 1)

            for n in range(4):
                shared_gelu(n, n % 2)

            def copy_rows(i, par):
                act.wait_ge(xT_ps, i + 1)
                wait(act, l1_ps, i - 1)
                nc.scalar.activation(xT[par], XTp[:, 0:EC * P].rearrange("p (c t) -> p c t", c=EC), ACT.Copy).then_inc(xT_sb, 1)

            def hidden_waits(i):
                act.wait_ge(t_ps, 2 * i + 2)
                wait(act, l2_ps, i - 1)

            def gelu(i, par):
                e = nc.scalar.value_load(tile_e[0:1, bass.ds(i, 1)], min_val=0, max_val=NE - 1)
                for f in range(FC):
                    last = nc.scalar.activation(hTe[par][:, f, :], HTp[:, f // 4, (f % 4) * P:(f % 4 + 1) * P], ACT.Gelu_apprx_tanh,
                                                bias=b1_s[:, bass.ds(e * FC + f, 1)])
                    if f % 4 == 3:
                        last.then_inc(hT_sb, 1)

            act.wait_ge(l2s_ps, 8)
            act.wait_ge(routed, 1)
            act.wait_ge(bias_in, 16 * 2)
            copy_rows(0, 0)
            copy_rows(1, 1)
            hidden_waits(0)
            copy_rows(2, 0)
            gelu(0, 0)

            def tile_step(half, k):
                i, par = half * 2 + 1 + k, (1 + k) % 2
                hidden_waits(i)
                copy_rows(i + 2, par)
                gelu(i, par)

            tiles_loop(act, tile_step)
            for i in range(TILES - 2, TILES):
                hidden_waits(i)
                gelu(i, i % 2)
            act.wait_ge(l2_ps, TILES)
            act.wait_ge(y_stored[0], 16 * ((TILES + 1) // 2))
            act.wait_ge(y_stored[1], 16 * (TILES // 2))
            with act.Fori(2, 4) as pair:
                for par in range(2):
                    shared_gelu(pair * 2 + par, par)

        @block.vector
        def _(dve):
            nc.vector.memset(mhalf, -0.5).then_inc(setup_dve, 1)

            def statistics(k):
                dve.wait_ge(x_in[k], 16)
                for b in range(4 * k, 4 * k + 4):
                    last = nc.vector.bn_stats(st1[:, b, :], xall[:, b, :])
                last.then_inc(var1, 1)
                dve.wait_ge(var1, 3 * k + 1)
                for b in range(4 * k, 4 * k + 4):
                    last = nc.vector.bn_aggr(mv1[:, b, :], st1[:, b, :])
                last.then_inc(var1, 1)
                dve.wait_ge(var1, 3 * k + 2)
                nc.vector.tensor_scalar(ve1[:, 4 * k:4 * k + 4], mv1[:, 4 * k:4 * k + 4, 1], EPS, None, ALU.add).then_inc(var1, 1)

            def normalise(b, par):
                nc.vector.tensor_scalar(xn[par], xall[:, bass.ds(b, 1), :].rearrange("t a e -> t (a e)"),
                                        mv1[:, bass.ds(b, 1), 0], rstd1[:, bass.ds(b, 1)], ALU.subtract, ALU.mult
                                        ).then_inc(xn_ready, 1)

            statistics(0)
            dve.wait_ge(rstd1_ready, 1)
            normalise(0, 0)
            normalise(1, 1)
            dve.wait_ge(setup_act, 2)
            dve.wait_ge(small_in, 16 * 3)
            nc.vector.tensor_scalar(bob, bob, tg[:, 0:1], None, ALU.mult).then_inc(setup_dve, 1)
            nc.vector.tensor_scalar(b2b, b2b, tg[:, 1:2], None, ALU.mult).then_inc(setup_dve, 1)

            def maximum(s, u):
                dve.wait_ge(qk_done, 6 * s.b + u + 1)
                nc.vector.tensor_reduce(mx[u % 2].rearrange("k (a h) -> k a h", a=2), S[u % 2].rearrange("k a (h q) -> k a h q", q=TQ),
                                        AX.X, ALU.max, negate=(u % 2 == 0)).then_inc(max_done, 1)
                if u % 2:
                    n = 6 * s.b + u
                    dve.wait_ge(max_done, n + 1)
                    wait(dve, pv_done, n + 1 - RING)
                    nc.vector.tensor_tensor(prob[ring(s.par, u)].rearrange("k (a h) q -> k a h q", a=2), S[1].rearrange("k a (h q) -> k a h q", q=TQ),
                                            mx[1].rearrange("k (a h) -> k a h", a=2).unsqueeze(3).to_broadcast([KR, 2, 4, TQ]),
                                            ALU.subtract).then_inc(sub_done, 1)

            def one_over_sum(b, par, u):
                n = 6 * b + u
                dve.wait_ge(exp_done, n + 1)
                if u % 2:
                    nc.vector.tensor_reduce(zz[1], prob[ring(par, u)], AX.X, ALU.add).then_inc(sum_done, 1)
                    dve.wait_ge(sum_done, 3 * b + (u + 1) // 2)
                wait(dve, vs_ready, n - 1)
                nc.vector.reciprocal(rz[u % 2], zz[u % 2]).then_inc(rz_ready, 1)

            def step(s):
                b, nxt, npar = s.b, s.b + 1, 1 - s.par
                attend, prep = s.has(0, B - 1), s.has(-1, B - 2)
                prev, prev2 = s.has(1, B), s.has(2, B + 1)
                first = isinstance(b, int) and b < 0
                if isinstance(b, int) and b == 0:
                    dve.wait_ge(cst_in, 16)
                if isinstance(b, int) and b in (2, 3):
                    dve.wait_ge(rstd1_ready, 2 if b == 2 else 4)
                for u in range(UNITS):
                    if u == 2 and isinstance(b, int) and b in (0, 1):
                        statistics(b + 2)
                    if u == 2 and prev:
                        dve.wait_ge(pv_done, 6 * b)
                        wait(dve, op_ps, b - 1)
                        Ov = O[:, 0:G * 2 * TQ].rearrange("p (g r q) -> p g r q", g=G, r=2)
                        nc.vector.tensor_scalar(otmp, Ov[:, :, 0, :], const("parmask")[:, 0:1], None, ALU.mult).then_inc(otmp_ready, 1)
                        dve.wait_ge(otmp_ready, b)
                        nc.vector.scalar_tensor_tensor(oT, Ov[:, :, 1, :], const("parmask")[:, 1:2], otmp, ALU.mult, ALU.add
                                                       ).then_inc(oT_ready, 1)
                    if u == 3 and prep:
                        dve.wait_ge(v_ps, 2 * nxt + 1)
                        wait(dve, vs_ready, 6 * b)
                        nc.vector.tensor_tensor(V[npar][:, 0:2, :], J[0][0:KR, :].rearrange("k (a e) -> k a e", a=2),
                                                bvb.unsqueeze(1).to_broadcast([KR, 2, E]), ALU.add).then_inc(v_sb, 1)
                    if u == 5 and prev:
                        xb = xall[:, bass.ds(b - 1, 1), :].rearrange("t a e -> t (a e)")
                        dve.wait_ge(op_ps, b)
                        dve.wait_ge(xbo_ready, b)
                        wait(dve, b2_added, b - 2)
                        nc.vector.scalar_tensor_tensor(x2[npar], J[2][0:TQ, 0:E], tg[:, 0:1], xb, ALU.mult, ALU.add).then_inc(x2_ready, 1)
                    if u == 5 and prep:
                        dve.wait_ge(v_ps, 2 * nxt + 2)
                        nc.vector.tensor_tensor(V[npar][:, 2, :], J[1][0:KR, 0:E], bvb, ALU.add).then_inc(v_sb, 1)
                    if u == 5 and prev:
                        dve.wait_ge(x2_ready, b)
                        nc.vector.bn_stats(st2, x2[npar]).then_inc(st2_ready, 1)
                        dve.wait_ge(st2_ready, b)
                    if attend:
                        maximum(s, u)
                    if u == 5 and prev:
                        nc.vector.bn_aggr(mv2, st2).then_inc(mv2_ready, 1)
                    if u == 0 and prev:
                        one_over_sum(b - 1, npar, 5)
                    if u > 0 and attend:
                        one_over_sum(b, s.par, u - 1)
                    if u == 5 and prev:
                        dve.wait_ge(mv2_ready, b)
                        nc.vector.tensor_scalar(ve2, mv2[:, 1:2], EPS, None, ALU.add).then_inc(ve2_ready, 1)
                    if u == 2 and s.has(0, B - 3):
                        dve.wait_ge(xnT_ps, b + 1)
                        normalise(b + 2, s.par)
                    if u == 2 and prev2:
                        dve.wait_ge(rstd2_ready, b - 1)
                        wait(dve, xn2_stored[s.par], (s.halves(-4) + 1) * 16)
                        nc.vector.tensor_scalar(xn2[s.par], x2[s.par], mv2[:, 0:1], rstd2, ALU.subtract, ALU.mult).then_inc(xn2_ready, 1)
                if first:
                    statistics(1)

            phase1(dve, step)

            steps = [0]

            def link(ins):
                steps[0] += 1
                ins.then_inc(rt, 1)
                dve.wait_ge(rt, steps[0])

            over_e = lambda v: v.unsqueeze(2).to_broadcast([TQ, B, NE])
            expert = route_const("expert").unsqueeze(1).to_broadcast([TQ, B, NE])
            dve.wait_ge(route_in, 16)
            dve.wait_ge(lg_ps, len(LOGITS))
            link(nc.vector.tensor_tensor(lg, J[1][0:TQ, 0:B * NE].rearrange("t (b e) -> t b e", e=NE),
                                         rbb.unsqueeze(1).to_broadcast([TQ, B, NE]), ALU.add))
            link(nc.vector.tensor_reduce(lmax, lg, AX.X, ALU.max))
            nc.vector.tensor_tensor(lg, lg, over_e(lmax), ALU.subtract).then_inc(rt_exp_in, 1)
            link(nc.vector.memset(ones_b, 1.0))
            link(nc.vector.tensor_copy(lower_b, route_const("lower")))
            dve.wait_ge(rt_exp, 1)
            link(nc.vector.tensor_reduce(lsum, pr, AX.X, ALU.add))
            link(nc.vector.reciprocal(lsum, lsum))
            link(nc.vector.tensor_tensor(pr, pr, over_e(lsum), ALU.mult))

            def choose(p, i, oh):
                link(nc.vector.tensor_reduce(p, pr, AX.X, ALU.max))
                link(nc.vector.tensor_tensor(t1, pr, over_e(p), ALU.is_equal))
                link(nc.vector.tensor_tensor(t1, t1, expert, ALU.mult))
                link(nc.vector.tensor_reduce(i, t1, AX.X, ALU.min))
                link(nc.vector.tensor_tensor(oh, expert, over_e(i), ALU.is_equal))

            choose(p1, i1, oh1)
            link(nc.vector.scalar_tensor_tensor(pr, oh1, -2.0, pr, ALU.mult, ALU.add))
            choose(p2, i2, oh2)
            nc.vector.tensor_tensor(hits.rearrange("t (b e) -> t b e", e=NE), oh1, oh2, ALU.add).then_inc(hits_ready, 1)
            link(nc.vector.tensor_tensor(lsum, p1, p2, ALU.add))
            link(nc.vector.reciprocal(lsum, lsum))
            for k, p in enumerate((p1, p2)):
                link(nc.vector.scalar_tensor_tensor(cw[:, k, :], p, tg[:, 1:2], lsum, ALU.mult, ALU.mult))
            dve.wait_ge(ranks_ps, 1)
            ranks = XTp[0:TQ, 0:(B + 1) * NE].rearrange("t (b e) -> t b e", e=NE)
            link(nc.vector.tensor_scalar(cnt_i, ranks[:, B, :], float(P - 1), None, ALU.add))
            link(nc.vector.tensor_scalar(cnt_i, cnt_i, 7, None, ALU.arith_shift_right))
            link(nc.vector.tensor_copy(cnt, cnt_i))
            link(nc.vector.tensor_tensor(prod, route_const("below").rearrange("t (a b) -> t a b", a=NE),
                                         cnt.unsqueeze(1).to_broadcast([TQ, NE, NE]), ALU.mult))
            link(nc.vector.tensor_reduce(end, prod, AX.X, ALU.add))
            link(nc.vector.tensor_tensor(base, end, cnt, ALU.subtract))
            link(nc.vector.tensor_scalar(base, base, float(P), None, ALU.mult))
            link(nc.vector.tensor_tensor(t1, ranks[:, 0:B, :], base.unsqueeze(1).to_broadcast([TQ, B, NE]), ALU.add))
            for k, oh in enumerate((oh1, oh2)):
                link(nc.vector.tensor_tensor(t2, t1, oh, ALU.mult))
                link(nc.vector.tensor_reduce(slot_f[:, :, k], t2, AX.X, ALU.add))
            link(nc.vector.tensor_copy(slot_i[:, :, :], slot_f))
            link(nc.vector.tensor_tensor(teq, route_const("tile")[0:1].unsqueeze(2).to_broadcast([1, TILES, NE - 1]),
                                         end[0:1, 0:NE - 1].unsqueeze(1).to_broadcast([1, TILES, NE - 1]), ALU.is_ge))
            link(nc.vector.tensor_reduce(tef, teq, AX.X, ALU.add))
            nc.vector.tensor_copy(tile_e[:, :], tef).then_inc(routed, 1)

            def shared_add(n):
                for k in range(2):
                    b = 2 * n + k
                    dve.wait_ge(l2s_ps, b + 1)
                    dve.wait_ge(b2_added, b + 1)
                    if b >= 12:
                        dve.wait_ge(comb2, b + 1)
                    nc.vector.scalar_tensor_tensor(xall[:, b, :], HTp[0:TQ, k, 0:E], tg[:, 1:2], xall[:, b, :], ALU.mult, ALU.add
                                                   ).then_inc(shared_done, 1)

            for n in range(4):
                shared_add(n)

            def copy_hidden(i, par):
                dve.wait_ge(l1_ps, i + 1)
                wait(dve, t_ps, 2 * i - 2)
                nc.vector.tensor_copy(h[par].rearrange("p (a n) -> p a n", a=2), Hp[par]).then_inc(h_sb, 1)

            def copy_result(i, half, par):
                e = nc.vector.value_load(tile_e[0:1, bass.ds(i, 1)], min_val=0, max_val=NE - 1)
                dve.wait_ge(l2_ps, i + 1)
                wait(dve, y_stored[par], half * 16)
                nc.vector.tensor_tensor(ys[par], Yp[:, 0:E], b2_s[:, bass.ds(e, 1), :].rearrange("p a n -> p (a n)"), ALU.add).then_inc(y_sb, 1)

            dve.wait_ge(routed, 1)
            dve.wait_ge(bias_in, 16 * 2)
            copy_hidden(0, 0)
            copy_hidden(1, 1)

            def tile_step(half, k):
                i, par = half * 2 + 1 + k, (1 + k) % 2
                copy_hidden(i + 1, 1 - par)
                copy_result(i - 1, half, 1 - par)

            tiles_loop(dve, tile_step)
            for i in range(TILES - 2, TILES + 1):
                if i + 1 < TILES:
                    copy_hidden(i + 1, (i + 1) % 2)
                copy_result(i - 1, (i - 1) // 2, (i - 1) % 2)

            def combine(b):
                dve.wait_ge(gathered[b], 16 * TOP)
                if b < 12:
                    dve.wait_ge(shared_done, b + 1)
                nc.vector.scalar_tensor_tensor(xall[:, b, :], yg[b][0], cw[:, 0, b:b + 1], xall[:, b, :], ALU.mult, ALU.add).then_inc(comb1, 1)
                dve.wait_ge(comb1, b + 1)
                nc.vector.scalar_tensor_tensor(xall[:, b, :], yg[b][1], cw[:, 1, b:b + 1], xall[:, b, :], ALU.mult, ALU.add).then_inc(comb2, 1)

            shared_add(4)
            shared_add(5)
            for b in range(12):
                combine(b)
            for b in range(12, B):
                combine(b)
            for n in range(6, 8):
                shared_add(n)

        @block.gpsimd
        def _(pool):
            nc.gpsimd.memset(zeros, 0.0).then_inc(zeroed, 1)
            pool.wait_ge(setup_dve, 1)

            def rstd_first(k):
                pool.wait_ge(var1, 3 * k + 3)
                nc.gpsimd.tensor_tensor(rstd1[:, 4 * k:4 * k + 4], ve1[:, 4 * k:4 * k + 4], mhalf.to_broadcast([TQ, 4]), ALU.pow
                                        ).then_inc(rstd1_ready, 1)

            rstd_first(0)
            pool.wait_ge(cst_in, 16)
            pool.wait_ge(setup_dve, 3)

            def scale_v(b, u, par):
                g, kt, n = u // KT, u % KT, 6 * b + u
                if kt == 0:
                    pool.wait_ge(v_sb, 2 * b + 2)
                wait(pool, pv_done, n + 1 - RING)
                pool.wait_ge(rz_ready, n + 1)
                nc.gpsimd.tensor_tensor(vs[ring(par, u)].rearrange("k (h d) -> k h d", h=HG), V[par][:, kt, g * P:(g + 1) * P].rearrange("k (h d) -> k h d", h=HG),
                                        rz[u % 2].unsqueeze(2).to_broadcast([KR, HG, D]), ALU.mult).then_inc(vs_ready, 1)

            def step(s):
                b, nxt, npar = s.b, s.b + 1, 1 - s.par
                attend, prep = s.has(0, B - 1), s.has(-1, B - 2)
                prev, prev2 = s.has(1, B), s.has(2, B + 1)
                if prev:
                    scale_v(b - 1, 5, npar)
                if attend:
                    scale_v(b, 0, s.par)
                    scale_v(b, 1, s.par)
                if prep:
                    xb = xall[:, bass.ds(nxt, 1), :].rearrange("t a e -> t (a e)")
                    pool.wait_ge(xn_ready, nxt + 1)
                    nc.gpsimd.tensor_tensor(xb, xb, bob, ALU.add).then_inc(xbo_ready, 1)
                if prep:
                    pool.wait_ge(qs_sb, nxt + 1)
                    wait(pool, qk_done, 6 * b)
                    for g in range(G):
                        nc.gpsimd.tensor_tensor(qbd[npar][:, g, :, :], qs[npar][:, g, :].unsqueeze(1).to_broadcast([P, HG, TQ]),
                                                       const("headmask").unsqueeze(2).to_broadcast([P, HG, TQ]), ALU.mult).then_inc(qbd_ready, 1)
                if attend:
                    scale_v(b, 2, s.par)
                    scale_v(b, 3, s.par)
                if prev2:
                    xb = xall[:, bass.ds(b - 2, 1), :].rearrange("t a e -> t (a e)")
                    pool.wait_ge(xn2_ready, b - 1)
                    nc.gpsimd.tensor_tensor(xb, x2[s.par], b2b, ALU.add).then_inc(b2_added, 1)
                if attend:
                    scale_v(b, 4, s.par)
                if prev:
                    pool.wait_ge(ve2_ready, b)
                    wait(pool, xn2_ready, b - 1)
                    nc.gpsimd.tensor_tensor(rstd2, ve2, mhalf, ALU.pow).then_inc(rstd2_ready, 1)
                if isinstance(b, int) and 0 <= b < 3:
                    rstd_first(b + 1)

            phase1(pool, step)
            pool.wait_ge(routed, 1)
            pool.wait_ge(slots_zeroed, 16)
            for b in range(B):
                pool.wait_ge(staged[b % 4], 16 * (b // 4 + 1))
                for k in range(TOP):
                    nc.gpsimd.indirect_dma_start(out=slots_d, out_offset=bass.IndirectOffsetOnAxis(ap=slot_i[:, b, k:k + 1], axis=0),
                                                 in_=stage[b % 4], in_offset=None).then_inc(scattered[b % 4], 16)
            pool.wait_ge(y_stored[0], 16 * ((TILES + 1) // 2))
            pool.wait_ge(y_stored[1], 16 * (TILES // 2))
            for b in range(B):
                for k in range(TOP):
                    nc.gpsimd.indirect_dma_start(out=yg[b][k], out_offset=None, in_=y_d,
                                                 in_offset=bass.IndirectOffsetOnAxis(ap=slot_i[:, b, k:k + 1], axis=0)).then_inc(gathered[b], 16)
    return nc


def _consts():
    import numpy as np

    c, r = np.zeros((P, CONST_W), np.float32), np.zeros((P, ROUTE_W), np.float32)
    p = np.arange(P)[:, None]

    def put(to, places, name, v):
        at, width = places[name]
        to[:, at:at + width] = v

    put(c, CONST, "ident", p == np.arange(P))
    put(c, CONST, "headmask", p // D == np.arange(HG))
    put(c, CONST, "parmask", (p // D) % 2 == np.arange(2))
    put(r, ROUTE, "lower", p < np.arange(TQ))
    put(r, ROUTE, "expert", np.arange(NE) - NE)
    put(r, ROUTE, "below", (np.arange(NE) <= np.arange(NE)[:, None]).reshape(1, -1))
    put(r, ROUTE, "tile", np.arange(TILES))
    return {"consts": c, "route": r}


def _layout(inp):
    import numpy as np

    f = {k: np.asarray(v) for k, v in inp.items()}
    rows = lambda a: np.ascontiguousarray(a.reshape(-1, P, a.shape[-1]).transpose(1, 0, 2))
    col = lambda a: np.ascontiguousarray(a.reshape(-1, P).T)

    def experts(w1, w2):
        a = w1.transpose(0, 2, 1).reshape(-1, EC, P, FF).transpose(0, 2, 1, 3).reshape(-1, P, EC * FF)
        b = w2.transpose(0, 2, 1).reshape(-1, FC, P, E).transpose(0, 2, 1, 3).reshape(-1, P, FC * E)
        ab = np.concatenate([a, b], axis=2).reshape(-1, P, 4, WE // 4).transpose(0, 2, 1, 3)
        return np.ascontiguousarray(ab.reshape(-1, P, WE // 4))

    ctxT = f["ctx_1024"].transpose(0, 2, 1).reshape(B, EC, P, TK).transpose(0, 2, 1, 3)
    return {
        "x": f["x"], "ctxT": np.ascontiguousarray(ctxT),
        "wq": rows(f["L0_xattn_Wq"]), "wkv": rows(f["L0_xattn_Wkv"]), "wo": rows(f["L0_xattn_Wo"]),
        "bq": col(f["L0_xattn_bq"]), "bk": col(f["L0_xattn_bkv"][:E]), "bv": f["L0_xattn_bkv"][E:], "bo": f["L0_xattn_bo"],
        "gates": np.concatenate([f["g_xattn"], f["g_ffn"]]),
        "w": experts(f["L0_ffn_spec_w1"], f["L0_ffn_spec_w2"]), "b1": col(f["L0_ffn_spec_b1"]), "b2": f["L0_ffn_spec_b2"].reshape(-1),
        "ws": experts(f["L0_ffn_shared_w1"][None], f["L0_ffn_shared_w2"][None]), "b1s": col(f["L0_ffn_shared_b1"]), "b2s": f["L0_ffn_shared_b2"],
        "rw": rows(np.ascontiguousarray(f["L0_ffn_router_w"].T)), "rb": f["L0_ffn_router_b"],
        **_consts(),
    }


def kernel(**inputs):
    import numpy as np
    import concourse.bacc as bacc
    from concourse.bass_utils import run_bass_kernel_spmd as run

    nc = bacc.Bacc("TRN2", target_bir_lowering=False, num_devices=1)
    arrays, args = {}, []
    for name, a in _layout(inputs).items():
        a = np.ascontiguousarray(a)
        arrays[f"in_{name}"] = a
        args.append(nc.dram_tensor(f"in_{name}", a.shape, mybir.dt.from_np(a.dtype), kind="ExternalInput").ap())
    args.append(nc.dram_tensor("out_0", (B, TQ, E), F32, kind="ExternalOutput").ap())
    build(nc, *args)
    r = run(nc, [arrays], core_ids=[0])
    return r.results[0]["out_0"]
```
